# Optimizing a Trainium2 kernel written in Bass

```python
import numpy as np
import jax
import jax.numpy as jnp

def _softmax(x, axis=-1):
    return jax.nn.softmax(x, axis=axis)

def _gelu(x):
    return jax.nn.gelu(x, approximate=True)

def _silu(x):
    return jax.nn.silu(x)

def _sigmoid(x):
    return jax.nn.sigmoid(x)

def _layernorm(x, axis=-1, eps=1e-05):
    m = jnp.mean(x, axis=axis, keepdims=True)
    v = jnp.var(x, axis=axis, keepdims=True)
    return (x - m) / jnp.sqrt(v + eps)

def _scatter_add(tgt, idx, src, axis=0):
    return tgt.at[idx].add(src)

def _segment_sum(src, seg, n):
    return jax.ops.segment_sum(src, seg, n)
kernel_name = 'mk_macaron_d1_jaxref_r8_4f45bb'

def setup_inputs(seed: int=0):
    np.random.seed(seed)
    _w = jnp.asarray

    def _L0_attn_setup():
        import jax, jax.numpy as jnp
        import numpy as np
        B, T, C = (8, 256, 128)
        NEG_INF = -1e+38

        def wkv(w, u, k, v):
            kt = jnp.swapaxes(k, 0, 1)
            vt = jnp.swapaxes(v, 0, 1)
            Bn, Cn = (k.shape[0], k.shape[2])
            aa = jnp.zeros((Bn, Cn), k.dtype)
            bb = jnp.zeros((Bn, Cn), k.dtype)
            pp = jnp.full((Bn, Cn), NEG_INF, k.dtype)

            def step(carry, kv):
                aa, bb, pp = carry
                kk, vv = kv
                ww = u + kk
                p = jnp.maximum(pp, ww)
                e1 = jnp.exp(pp - p)
                e2 = jnp.exp(ww - p)
                y = (e1 * aa + e2 * vv) / (e1 * bb + e2)
                ww2 = pp + w
                p2 = jnp.maximum(ww2, kk)
                e1 = jnp.exp(ww2 - p2)
                e2 = jnp.exp(kk - p2)
                return ((e1 * aa + e2 * vv, e1 * bb + e2, p2), y)
            _, y = jax.lax.scan(step, (aa, bb, pp), (kt, vt))
            return jnp.swapaxes(y, 0, 1)
        key = jax.random.key(seed)
        ks = jax.random.split(key, 10)
        s = 1.0 / np.sqrt(C)
        return {'x': jax.random.normal(ks[0], (B, T, C), jnp.float32), 'time_decay': jax.random.normal(ks[1], (C,), jnp.float32), 'time_first': jax.random.normal(ks[2], (C,), jnp.float32), 'time_mix_k': jax.random.uniform(ks[3], (1, 1, C), jnp.float32), 'time_mix_v': jax.random.uniform(ks[4], (1, 1, C), jnp.float32), 'time_mix_r': jax.random.uniform(ks[5], (1, 1, C), jnp.float32), 'Wk': jax.random.normal(ks[6], (C, C), jnp.float32) * s, 'Wv': jax.random.normal(ks[7], (C, C), jnp.float32) * s, 'Wr': jax.random.normal(ks[8], (C, C), jnp.float32) * s, 'Wo': jax.random.normal(ks[9], (C, C), jnp.float32) * s}
    _L0_attn_in = _L0_attn_setup()

    def _L0_ffn_setup():
        import jax, jax.numpy as jnp
        import numpy as np
        B, T, DIM, H, DH, TOPK = (4, 256, 128, 8, 64, 3)
        key = jax.random.key(seed)
        ks = jax.random.split(key, 6)
        x = jax.random.normal(ks[0], (B, T, DIM), dtype=jnp.float32)
        sc = 1.0 / np.sqrt(DIM)
        Wq = jax.random.normal(ks[1], (DIM, H * DH), dtype=jnp.float32) * sc
        Wkv = jax.random.normal(ks[2], (DIM, 2 * H * DH), dtype=jnp.float32) * sc
        Ws = jax.random.normal(ks[3], (DIM, H), dtype=jnp.float32) * sc
        Wo = jax.random.normal(ks[4], (H, DH, DIM), dtype=jnp.float32) * (1.0 / np.sqrt(DH))
        bo = jax.random.normal(ks[5], (H, DIM), dtype=jnp.float32) * 0.01
        return {'x': x, 'Wq': Wq, 'Wkv': Wkv, 'Ws': Ws, 'Wo': Wo, 'bo': bo}
    _L0_ffn_in = _L0_ffn_setup()
    _d = {'L0_attn_x': _L0_attn_in['x'], 'L0_attn_time_decay': _L0_attn_in['time_decay'], 'L0_attn_time_first': _L0_attn_in['time_first'], 'L0_attn_time_mix_k': _L0_attn_in['time_mix_k'], 'L0_attn_time_mix_v': _L0_attn_in['time_mix_v'], 'L0_attn_time_mix_r': _L0_attn_in['time_mix_r'], 'L0_attn_Wk': _L0_attn_in['Wk'], 'L0_attn_Wv': _L0_attn_in['Wv'], 'L0_attn_Wr': _L0_attn_in['Wr'], 'L0_attn_Wo': _L0_attn_in['Wo'], 'L0_ffn_Wq': _L0_ffn_in['Wq'], 'L0_ffn_Wkv': _L0_ffn_in['Wkv'], 'L0_ffn_Ws': _L0_ffn_in['Ws'], 'L0_ffn_Wo': _L0_ffn_in['Wo'], 'L0_ffn_bo': _L0_ffn_in['bo']}
    _x0 = _d['L0_attn_x']
    _d['L0_attn_x'] = jax.random.normal(jax.random.fold_in(jax.random.key(seed), 1), (8, 1024, 128), dtype=_x0.dtype)
    del _x0
    return _d

def reference(L0_attn_x, L0_attn_time_decay, L0_attn_time_first, L0_attn_time_mix_k, L0_attn_time_mix_v, L0_attn_time_mix_r, L0_attn_Wk, L0_attn_Wv, L0_attn_Wr, L0_attn_Wo, L0_ffn_Wq, L0_ffn_Wkv, L0_ffn_Ws, L0_ffn_Wo, L0_ffn_bo):

    def _L0_attn_ref(x, time_decay, time_first, time_mix_k, time_mix_v, time_mix_r, Wk, Wv, Wr, Wo):
        import jax, jax.numpy as jnp
        import numpy as np
        B, T, C = (8, 256, 128)
        NEG_INF = -1e+38

        def wkv(w, u, k, v):
            kt = jnp.swapaxes(k, 0, 1)
            vt = jnp.swapaxes(v, 0, 1)
            Bn, Cn = (k.shape[0], k.shape[2])
            aa = jnp.zeros((Bn, Cn), k.dtype)
            bb = jnp.zeros((Bn, Cn), k.dtype)
            pp = jnp.full((Bn, Cn), NEG_INF, k.dtype)

            def step(carry, kv):
                aa, bb, pp = carry
                kk, vv = kv
                ww = u + kk
                p = jnp.maximum(pp, ww)
                e1 = jnp.exp(pp - p)
                e2 = jnp.exp(ww - p)
                y = (e1 * aa + e2 * vv) / (e1 * bb + e2)
                ww2 = pp + w
                p2 = jnp.maximum(ww2, kk)
                e1 = jnp.exp(ww2 - p2)
                e2 = jnp.exp(kk - p2)
                return ((e1 * aa + e2 * vv, e1 * bb + e2, p2), y)
            _, y = jax.lax.scan(step, (aa, bb, pp), (kt, vt))
            return jnp.swapaxes(y, 0, 1)
        xx = jnp.pad(x, ((0, 0), (1, 0), (0, 0)))[:, :-1, :]
        xk = x * time_mix_k + xx * (1.0 - time_mix_k)
        xv = x * time_mix_v + xx * (1.0 - time_mix_v)
        xr = x * time_mix_r + xx * (1.0 - time_mix_r)
        k = jnp.einsum('btc,dc->btd', xk, Wk)
        v = jnp.einsum('btc,dc->btd', xv, Wv)
        r = jnp.einsum('btc,dc->btd', xr, Wr)
        w = -jnp.exp(time_decay)
        rwkv = jax.nn.sigmoid(r) * wkv(w, time_first, k, v)
        return jnp.einsum('btc,dc->btd', rwkv, Wo)

    def _L0_ffn_ref(x, Wq, Wkv, Ws, Wo, bo):
        import jax, jax.numpy as jnp
        import numpy as np
        B, T, DIM, H, DH, TOPK = (4, 256, 128, 8, 64, 3)
        b, t, _ = x.shape
        s = jax.nn.sigmoid(x @ Ws)
        vals, idx = jax.lax.top_k(s, TOPK)
        bi = jnp.arange(b)[:, None, None]
        ti = jnp.arange(t)[None, :, None]
        scores = jnp.zeros_like(s).at[bi, ti, idx].set(vals)
        q = (x @ Wq).reshape(b, t, H, DH).transpose(0, 2, 1, 3)
        kv = (x @ Wkv).reshape(b, t, 2, H, DH).transpose(2, 0, 3, 1, 4)
        k, v = (kv[0], kv[1])
        scale = DH ** (-0.5)
        attn = jax.nn.softmax(jnp.einsum('bhid,bhjd->bhij', q * scale, k), axis=-1)
        out = jnp.einsum('bhij,bhjd->bhid', attn, v)
        proj = jnp.einsum('bhtd,hde->bhte', out, Wo) + bo[None, :, None, :]
        return jnp.einsum('bhte,bth->bte', proj, scores)
    x = L0_attn_x
    x = x + 0.5 * _L0_ffn_ref(_layernorm(x, axis=-1), L0_ffn_Wq, L0_ffn_Wkv, L0_ffn_Ws, L0_ffn_Wo, L0_ffn_bo)
    x = x + _L0_attn_ref(_layernorm(x, axis=-1), L0_attn_time_decay, L0_attn_time_first, L0_attn_time_mix_k, L0_attn_time_mix_v, L0_attn_time_mix_r, L0_attn_Wk, L0_attn_Wv, L0_attn_Wr, L0_attn_Wo)
    x = x + 0.5 * _L0_ffn_ref(_layernorm(x, axis=-1), L0_ffn_Wq, L0_ffn_Wkv, L0_ffn_Ws, L0_ffn_Wo, L0_ffn_bo)
    return x

_drawn_inputs = setup_inputs


def setup_inputs(seed=0):
    import zlib

    import numpy as np

    out = dict(_drawn_inputs(seed))
    spreads = {}
    factors = {'L0_ffn_bo': 4.588}
    for name, (base, spread) in spreads.items():
        noise = np.random.default_rng([zlib.crc32(name.encode()), seed]).standard_normal(out[name].shape)
        drawn = base * np.exp(spread * noise) if base else spread * noise
        out[name] = jnp.asarray(drawn.astype(out[name].dtype))
    for name, factor in factors.items():
        out[name] = (out[name] * factor).astype(out[name].dtype)
    return out
```

```python
from contextlib import ExitStack

import concourse.bass as bass
from concourse import mybir

F32 = mybir.dt.float32
F32R = mybir.dt.float32r
BF16 = mybir.dt.bfloat16
I32 = mybir.dt.int32
U32 = mybir.dt.uint32
ALU = mybir.AluOpType
ACT = mybir.ActivationFunctionType
AX = mybir.AxisListType

P = 128
NB, T, C = 8, 1024, 128
NT = T // P
H, DH, TOPK = 8, 64, 3
NS = (TOPK * T + H * (P - 1)) // P
SLOTS = NS * P
EPS = 1e-5
NEG_INF = -1e38
SCALE = DH ** -0.5

LN_CHAIN, GATE_CHAIN, WKV_CHAIN = 1, 34, 15


class Chain:

    def __init__(self, eng, sem, start):
        self.eng, self.sem, self.start, self.n = eng, sem, start, 0

    def done(self, ins):
        self.n += 1
        ins.then_inc(self.sem, 1)

    def wait(self):
        self.eng.wait_ge(self.sem, self.start + self.n)

    def link(self, ins):
        self.done(ins)
        self.wait()


def build(nc, x_in, time_decay, time_first, mix_k, mix_v, mix_r, rk_w, rv_w, rr_w, ro_w,
          q_w, kv_w, s_w, o_w, o_b, out):
    ctx = ExitStack()
    with ctx:
        def sb(name, shape, dt=F32):
            return ctx.enter_context(nc.sbuf_tensor(name, shape, dt))

        def sem(name):
            return ctx.enter_context(nc.semaphore(name))

        x_slots = nc.dram_tensor("x_slots", (SLOTS, C), F32, kind="Internal").ap()
        y_slots = nc.dram_tensor("y_slots", (SLOTS, C), F32, kind="Internal").ap()

        x = sb("x", [P, NB * T])
        A_hi = sb("A_hi", [P, H * T], F32R)
        A_lo = sb("A_lo", [P, H * T], F32R)
        V = sb("V", [P, NT * H * DH])
        xn = sb("xn", [P, NT * C])
        xT = sb("xT", [P, 1 + T])
        work = sb("work", [P, 11 * (T + 2)])
        xs = sb("xs", [P, 2, C])
        xs_hi = sb("xs_hi", [P, 2, P], F32R)
        xs_lo = sb("xs_lo", [P, 2, P], F32R)
        o_sb = sb("o_sb", [P, 2, DH])
        oT = sb("oT", [DH + 1, 2, P])
        y_sb = sb("y_sb", [P, 2, C])
        mx = sb("mx", [P, 2])
        den = sb("den", [P, NS + 1])
        rden = sb("rden", [P, 2])
        GT = sb("GT", [P, H, C])
        wv = sb("wv", [P, H * DH])
        wo = sb("wo", [DH + 1, H * C])
        ws = sb("ws", [P, H])
        ident = sb("ident", [P, P])
        tri = sb("tri", [P, P], BF16)
        ones = sb("ones", [P, P], BF16)
        ones_f = sb("ones_f", [P, P])
        lower = sb("lower", [P, H, H])
        iota_i = sb("iota_i", [P, 32 * H], I32)
        steps = sb("steps", [P, H, H])
        tile_no = sb("tile_no", [1, 32, H])
        stats = sb("stats", [P, NT, 6])
        mv = sb("mv", [P, NT, 2])
        rstd = sb("rstd", [P, 2, NT])
        powr = sb("powr", [P, NT])
        eg = sb("eg", [P, NT * H])
        sg = sb("sg", [P, NT, H])
        cmp1 = sb("cmp1", [P, NT, H, H])
        cmp2 = sb("cmp2", [P, NT, H, H])
        small = sb("small", [P, 8, NT, H])
        mask_b = sb("mask_b", [P, NT, H], BF16)
        nh = sb("nh", [P, 4, H])
        slot_i = sb("slot_i", [P, TOPK, NT], U32)
        slot_f = sb("slot_f", [P, TOPK, NT])
        gate = sb("gate", [P, TOPK, NT])
        head_f = sb("head_f", [1, 32])
        head_i = sb("head_i", [1, 32], I32)
        headcmp = sb("headcmp", [1, 32, H])
        rw_raw = sb("rw_raw", [P, 4, C])
        rw_T = sb("rw_T", [P, 4, C])
        cols = sb("cols", [P, 6])
        w_rows = sb("w_rows", [P, T])

        probs = work[:, 0:2 * T].rearrange("p (a k) -> p a k", a=2)
        probsT = work[:, 2 * T:4 * T].rearrange("p (a k) -> p a k", a=2)
        y_got = work[:, 4 * T:7 * T].rearrange("p (j n c) -> p j n c", j=TOPK, n=NT)
        wq_raw = work[:, 0:512]
        wk_raw = work[:, 512:1024]
        wqT = work[0:DH, 1024:2048].rearrange("p (h c) -> p h c", h=H)
        wkT = work[0:DH, 2048:3072].rearrange("p (h c) -> p h c", h=H)

        A_zero = work[:, 4 * T:4 * T + NS * C]

        def area(i, n=T):
            return work[:, i * (T + 2):i * (T + 2) + n]

        S = ctx.enter_context(nc.psum_tensor("S", [P, 2, T], F32))
        TP = ctx.enter_context(nc.psum_tensor("TP", [P, T], F32))
        OB = ctx.enter_context(nc.psum_tensor("OB", [P, 512], F32))
        MB = ctx.enter_context(nc.psum_tensor("MB", [P, 512], F32))
        xT_ps, oT_ps, y_ps = MB[:, 0:128], MB[0:DH, 128:256], MB[:, 256:384]
        logit_ps, rank_ps, count_ps = MB[:, 384:448], MB[:, 448:512], OB[:, 448:456]

        loaded = sem("loaded")
        zeroed = sem("zeroed")
        consts = sem("consts")
        pool_setup = sem("pool_setup")
        w_turned = sem("w_turned")
        w_copied = sem("w_copied")
        g_made = sem("g_made")
        g_copied = sem("g_copied")
        rw_copied = sem("rw_copied")
        cols_made = sem("cols_made")
        mv_made = sem("mv_made")
        rstd_made = sem("rstd_made")
        xn_made = sem("xn_made")
        xn_turned = sem("xn_turned")
        xT_made = sem("xT_made")
        logits_made = sem("logits_made")
        eg_made = sem("eg_made")
        mask_made = sem("mask_made")
        rank_made = sem("rank_made")
        slots_made = sem("slots_made")
        scattered = sem("scattered")
        a_made = sem("a_made")
        a_hi_made = sem("a_hi_made")
        a_lo_made = sem("a_lo_made")
        v_made = sem("v_made")
        v_copied = sem("v_copied")
        xs_loaded = [sem(f"xs_loaded{i}") for i in range(2)]
        xs_turned = sem("xs_turned")
        xs_hi_made = sem("xs_hi_made")
        xs_lo_made = sem("xs_lo_made")
        s_made = sem("s_made")
        max_made = sem("max_made")
        p_made = sem("p_made")
        p_turned = sem("p_turned")
        pT_a = sem("pT_a")
        pT_b = sem("pT_b")
        o_made = sem("o_made")
        rden_made = sem("rden_made")
        o_normed = sem("o_normed")
        o_turned = sem("o_turned")
        oT_copied = sem("oT_copied")
        y_made = sem("y_made")
        y_copied = sem("y_copied")
        y_stored = [sem(f"y_stored{i}") for i in range(2)]
        y_gathered = sem("y_gathered")
        ffn_done = sem("ffn_done")
        mixed = sem("mixed")
        kvr_made = sem("kvr_made")
        kvr_copied = sem("kvr_copied")
        arg_made = sem("arg_made")
        exp_made = sem("exp_made")
        rw_made = sem("rw_made")
        ro_made = sem("ro_made")
        wkv_done = sem("wkv_done")
        ln_chain = sem("ln_chain")
        gate_chain = sem("gate_chain")
        wkv_chain = sem("wkv_chain")
        add_chain = sem("add_chain")
        pow_chain = sem("pow_chain")
        stored = sem("stored")
        passed = sem("passed")

        NCONST = 13
        NLOAD = NB + 6 + 4 + 5

        block = ctx.enter_context(nc.Block())

        @block.sync
        def _(sp):
            for b in range(NB):
                sp.dma_start(x[:, b * T:(b + 1) * T].rearrange("p (n c) -> p n c", c=C),
                             x_in[b].rearrange("(n p) c -> p n c", p=P)).then_inc(loaded, 16)
            sp.dma_start(wq_raw, q_w).then_inc(loaded, 16)
            sp.dma_start(wk_raw, kv_w[:, 0:512]).then_inc(loaded, 16)
            sp.dma_start(wv[:, :], kv_w[:, 512:1024]).then_inc(loaded, 16)
            sp.dma_start(ws[:, :], s_w).then_inc(loaded, 16)
            sp.dma_start(wo[0:DH, :].rearrange("d (h e) -> d h e", h=H), o_w.rearrange("h d e -> d h e")).then_inc(loaded, 16)
            sp.dma_start(wo[DH:DH + 1, :], o_b.rearrange("(o h) e -> o (h e)", o=1)).then_inc(loaded, 16)
            for i, w in enumerate((rk_w, rv_w, rr_w, ro_w)):
                sp.dma_start(rw_raw[:, i, :], w).then_inc(loaded, 16)
            for i, v in enumerate((time_decay, time_first)):
                sp.dma_start(cols[:, i:i + 1], v.rearrange("(c o) -> c o", o=1)).then_inc(loaded, 16)
            for i, v in enumerate((mix_k, mix_v, mix_r)):
                sp.dma_start(cols[:, 2 + i:3 + i], v.rearrange("a b c -> c (a b)")).then_inc(loaded, 16)
            sp.wait_ge(pool_setup, 1)
            sp.dma_start(x_slots.rearrange("(n p) c -> p n c", p=P),
                         A_zero.rearrange("p (n c) -> p n c", c=C)).then_inc(zeroed, 16)

            def slot_tile(f, t, par):
                if not isinstance(t, int) or t >= 2:
                    sp.wait_ge(xs_turned, f * NS + t - 1)
                sp.dma_start(xs[:, par, :], x_slots[bass.ds(t * P, P), :]).then_inc(xs_loaded[par], 16)

            def y_store(f, t, par):
                sp.wait_ge(y_copied, f * NS + t + 1)
                sp.dma_start(y_slots[bass.ds(t * P, P), :], y_sb[:, par, :]).then_inc(y_stored[par], 16)

            def ffn(layer):
                with sp.Fori(0, NB) as b:
                    f = b + layer * NB
                    sp.wait_ge(scattered, (f + 1) * (TOPK * NT * 16))
                    for t in range(6):
                        slot_tile(f, t, t % 2)
                        if t == 5:
                            y_store(f, 0, 0)
                    with sp.Fori(0, 12) as i:
                        for par in range(2):
                            slot_tile(f, i * 2 + (6 + par), par)
                            y_store(f, i * 2 + (1 + par), 1 - par)
                    slot_tile(f, NS - 1, 0)
                    for t in range(25, NS):
                        y_store(f, t, t % 2)

            ffn(0)
            ffn(1)
            sp.wait_ge(ffn_done, 2 * NB)
            for b in range(NB):
                sp.dma_start(out[b].rearrange("(n p) c -> p n c", p=P),
                             x[:, b * T:(b + 1) * T].rearrange("p (n c) -> p n c", c=C)).then_inc(stored, 16)
            sp.wait_ge(stored, 16 * NB)

        @block.gpsimd
        def _(pool):
            pool.memset(A_zero, 0.0).then_inc(pool_setup, 1)
            pool.memset(ones_f[:, :], 1.0).then_inc(consts, 1)
            pool.memset(ones[:, :], 1.0).then_inc(consts, 1)
            pool.memset(powr[:, :], -0.5).then_inc(consts, 1)
            pool.memset(xT[:, 0:1], 0.0).then_inc(consts, 1)
            pool.memset(cmp1[:, 0], 1.0).then_inc(consts, 1)
            pool.wait_ge(consts, 6)
            pool.affine_select(out=ident[:, :], in_=ones_f[:, :], compare_op=ALU.is_equal, fill=0.0, base=0,
                               pattern=[[-1, P]], channel_multiplier=1).then_inc(consts, 1)
            pool.affine_select(out=tri[:, :], in_=ones[:, :], compare_op=ALU.is_gt, fill=0.0, base=0,
                               pattern=[[1, P]], channel_multiplier=-1).then_inc(consts, 1)
            pool.affine_select(out=lower[:, :, :], in_=cmp1[:, 0], compare_op=ALU.is_gt, fill=0.0, base=0,
                               pattern=[[1, H], [-1, H]], channel_multiplier=0).then_inc(consts, 1)
            pool.iota(iota_i[:, 0:H * H], [[0, H], [P, H]], base=0, channel_multiplier=0).then_inc(consts, 1)
            pool.wait_ge(consts, 10)
            pool.tensor_copy(steps[:, :, :].rearrange("p a b -> p (a b)"), iota_i[:, 0:H * H]).then_inc(consts, 1)
            pool.wait_ge(consts, 11)
            pool.iota(iota_i[:, :], [[1, 32], [0, H]], base=0, channel_multiplier=0).then_inc(consts, 1)
            pool.wait_ge(consts, 12)
            pool.tensor_copy(tile_no[:, :, :].rearrange("p a b -> p (a b)"), iota_i[0:1, :]).then_inc(consts, 1)

            def root(r):
                pool.wait_ge(mv_made, r + 1)
                pool.sem_inc(passed, 1)
                pool.tensor_scalar(rstd[:, 0, :], mv[:, :, 1], EPS, None, ALU.add).then_inc(pow_chain, 1)
                pool.wait_ge(pow_chain, r + 1)
                pool.tensor_tensor(rstd[:, 1, :], rstd[:, 0, :], powr[:, :], ALU.pow).then_inc(rstd_made, 1)

            def ffn(layer):
                with pool.Fori(0, NB) as b:
                    f = b + layer * NB
                    root(f + layer * NB)
                    pool.wait_ge(slots_made, f + 1)
                    pool.sem_inc(passed, 1)
                    for j in range(TOPK):
                        for n in range(NT):
                            pool.indirect_dma_start(
                                out=x_slots, out_offset=bass.IndirectOffsetOnAxis(ap=slot_i[:, j, n:n + 1], axis=0),
                                in_=xn[:, n * C:(n + 1) * C], in_offset=None).then_inc(scattered, 16)
                    pool.wait_ge(y_stored[0], (f + 1) * (16 * 16))
                    pool.wait_ge(y_stored[1], (f + 1) * (15 * 16))
                    pool.sem_inc(passed, 1)
                    for j in range(TOPK):
                        for n in range(NT):
                            pool.indirect_dma_start(
                                out=y_got[:, j, n, :], out_offset=None, in_=y_slots,
                                in_offset=bass.IndirectOffsetOnAxis(ap=slot_i[:, j, n:n + 1], axis=0)).then_inc(y_gathered, 16)
                    pool.wait_ge(ffn_done, f + 1)

            pool.wait_ge(zeroed, 16)
            ffn(0)
            with pool.Fori(0, NB) as b:
                root(b + NB)
            ffn(1)

        @block.scalar
        def _(act):
            act.wait_ge(w_turned, 1)
            act.activation(wqT.rearrange("p h c -> p (h c)"), S[0:DH, 0, :], ACT.Copy).then_inc(w_copied, 1)
            act.activation(wkT.rearrange("p h c -> p (h c)"), S[0:DH, 1, :], ACT.Copy).then_inc(w_copied, 1)
            act.activation(rw_T[:, :, :].rearrange("p a b -> p (a b)"), TP[:, 0:512], ACT.Copy).then_inc(rw_copied, 1)
            act.wait_ge(g_made, 1)
            act.activation(GT[:, :, :].rearrange("p h c -> p (h c)"), S[:, 0, :], ACT.Copy, scale=SCALE).then_inc(g_copied, 1)
            act.wait_ge(loaded, 16 * NLOAD)
            act.activation(cols[:, 5:6], cols[:, 0:1], ACT.Exp).then_inc(cols_made, 1)

            def transpose_out(r):
                act.wait_ge(xn_turned, r + 1)
                act.activation(xT[:, 1:1 + T], S[:, 0, :], ACT.Copy).then_inc(xT_made, 1)

            def gates(f):
                act.wait_ge(logits_made, f + 1)
                act.activation(eg[:, :], logit_ps, ACT.Exp, scale=-1.0).then_inc(eg_made, 1)

            def keys_values(f):
                for h in range(H):
                    act.wait_ge(a_made, f * H + (h + 1))
                    act.activation(A_hi[:, h * T:(h + 1) * T], S[:, h % 2, :], ACT.Copy).then_inc(a_hi_made, 1)
                for n in range(NT):
                    act.wait_ge(v_made, f * NT + (n + 1))
                    act.activation(V[:, n * 512:(n + 1) * 512], TP[:, (n % 2) * 512:(n % 2) * 512 + 512],
                                   ACT.Copy).then_inc(v_copied, 1)

            def oT_copy(f, t, par):
                act.wait_ge(o_turned, f * NS + t + 1)
                act.activation(oT[0:DH, par, :], oT_ps, ACT.Copy).then_inc(oT_copied, 1)

            def pT_copy(f, t, par):
                act.wait_ge(p_turned, (f * NS + t) * 2 + 1)
                if not isinstance(t, int) or t >= 2:
                    act.wait_ge(o_made, f * NS + t - 1)
                act.activation(probsT[:, par, 0:512], TP[:, 0:512], ACT.Copy).then_inc(pT_a, 1)

            def exps(f, t, par):
                act.wait_ge(max_made, f * NS + t + 1)
                if not isinstance(t, int) or t >= 2:
                    act.wait_ge(p_turned, (f * NS + t) * 2 - 2)
                act.activation(probs[:, par, :], S[:, par, :], ACT.Exp, bias=mx[:, par:par + 1],
                               accum_out=den[:, bass.ds(t, 1)]).then_inc(p_made, 1)

            def x_hi(f, t, par):
                act.wait_ge(xs_turned, f * NS + t + 1)
                if not isinstance(t, int) or t >= 2:
                    act.wait_ge(s_made, f * NS + t - 1)
                act.activation(xs_hi[:, par, :], xT_ps, ACT.Copy).then_inc(xs_hi_made, 1)

            def step(f, s, par, first=0, last=NS - 1):
                live = lambda t: first <= t <= last
                k = 5 if not isinstance(s, int) else s
                if live(k - 2):
                    oT_copy(f, s - 2, par)
                if live(k):
                    pT_copy(f, s, par)
                if live(k + 2):
                    x_hi(f, s + 2, par)
                if live(k + 1):
                    exps(f, s + 1, 1 - par)

            def ffn(layer):
                with act.Fori(0, NB) as b:
                    f = b + layer * NB
                    transpose_out(f + layer * NB)
                    gates(f)
                    keys_values(f)
                    for s in range(-2, 4):
                        step(f, s, s % 2)
                    with act.Fori(0, 12) as i:
                        for par in range(2):
                            step(f, i * 2 + (4 + par), par)
                    for s in range(28, NS + 2):
                        step(f, s, s % 2)

            ffn(0)
            with act.Fori(0, NB) as b:
                transpose_out(b + NB)
                for i, (dst, src) in enumerate(((area(4), S[:, 0, :]), (area(5), S[:, 1, :]))):
                    act.wait_ge(kvr_made, b * 3 + (i + 1))
                    act.activation(dst, src, ACT.Copy).then_inc(kvr_copied, 1)
                act.wait_ge(kvr_made, b * 3 + 3)
                act.activation(area(6), TP[:, :], ACT.Exp, scale=-1.0).then_inc(kvr_copied, 1)
                for i, a in enumerate((1, 2, 3, 7)):
                    act.wait_ge(arg_made, b * 4 + (i + 1))
                    act.activation(area(a), area(a), ACT.Exp).then_inc(exp_made, 1)
            ffn(1)

        @block.vector
        def _(dve):
            dve.memset(oT[DH:DH + 1, :, :], 1.0).then_inc(consts, 1)
            dve.wait_ge(cols_made, 1)
            dve.wait_ge(consts, NCONST)
            dve.tensor_scalar(cols[:, 5:6], cols[:, 5:6], -1.0, None, ALU.mult).then_inc(cols_made, 1)
            dve.wait_ge(cols_made, 2)
            dve.memset(w_rows[:, :], 0.0).then_inc(cols_made, 1)
            dve.wait_ge(cols_made, 3)
            dve.tensor_scalar(w_rows[:, :], w_rows[:, :], cols[:, 5:6], None, ALU.add).then_inc(cols_made, 1)

            def norm(b, r):
                ch = Chain(dve, ln_chain, r * LN_CHAIN)
                for n in range(NT):
                    ins = dve.bn_stats(stats[:, n, :], x[:, bass.ds(b * T + n * C, C)])
                ch.done(ins)
                ch.wait()
                dve.sem_inc(passed, 1)
                for n in range(NT):
                    ins = dve.bn_aggr(mv[:, n, :], stats[:, n, :])
                ins.then_inc(mv_made, 1)
                dve.wait_ge(rstd_made, r + 1)
                for n in range(NT):
                    ins = dve.tensor_scalar(xn[:, n * C:(n + 1) * C], x[:, bass.ds(b * T + n * C, C)],
                                            mv[:, n, 0:1], rstd[:, 1, n:n + 1], ALU.subtract, ALU.mult)
                ins.then_inc(xn_made, 1)

            def gates(f):
                ch = Chain(dve, gate_chain, f * GATE_CHAIN)
                dve.wait_ge(eg_made, f + 1)
                flat = lambda ap: ap.rearrange("p a b -> p (a b)")
                ch.link(dve.tensor_scalar(eg[:, :], eg[:, :], 1.0, None, ALU.add))
                ch.link(dve.reciprocal(flat(sg[:, :, :]), eg[:, :]))
                g_of = sg[:, :, :].unsqueeze(2).broadcast_to([P, NT, H, H])
                h_of = sg[:, :, :].unsqueeze(3).broadcast_to([P, NT, H, H])
                low = lower[:, :, :].unsqueeze(1).broadcast_to([P, NT, H, H])
                ch.done(dve.tensor_tensor(cmp1[:, :, :, :], g_of, h_of, ALU.is_equal))
                ch.link(dve.tensor_tensor(cmp2[:, :, :, :], g_of, h_of, ALU.is_gt))
                ch.link(dve.tensor_tensor(cmp1[:, :, :, :], cmp1[:, :, :, :], low, ALU.mult))
                ch.link(dve.tensor_tensor(cmp1[:, :, :, :], cmp1[:, :, :, :], cmp2[:, :, :, :], ALU.add))
                ch.link(dve.tensor_reduce(small[:, 0], cmp1[:, :, :, :], AX.X, ALU.add))
                ch.link(dve.tensor_scalar(small[:, 1], small[:, 0], float(TOPK), None, ALU.is_lt))
                dve.tensor_copy(mask_b[:, :, :], small[:, 1]).then_inc(mask_made, 1)
                m_of = small[:, 1].unsqueeze(2).broadcast_to([P, NT, H, H])
                ch.link(dve.tensor_tensor(cmp2[:, :, :, :], m_of, low, ALU.mult))
                ch.link(dve.tensor_reduce(small[:, 2], cmp2[:, :, :, :], AX.X, ALU.add))
                dve.wait_ge(rank_made, f + 1)
                ch.link(dve.tensor_copy(nh[:, 0], count_ps))
                n_of = nh[:, 0].unsqueeze(2).broadcast_to([P, H, H])
                ch.link(dve.tensor_tensor(cmp1[:, 0], n_of, steps[:, :, :], ALU.is_gt))
                ch.link(dve.tensor_reduce(nh[:, 1], cmp1[:, 0], AX.X, ALU.add))
                ch.link(dve.tensor_tensor(cmp1[:, 0], nh[:, 1].unsqueeze(1).broadcast_to([P, H, H]),
                                          lower[:, :, :], ALU.mult))
                ch.link(dve.tensor_reduce(nh[:, 2], cmp1[:, 0], AX.X, ALU.add))
                ch.link(dve.tensor_tensor(headcmp[:, :, :], tile_no[:, :, :],
                                          nh[0:1, 2].unsqueeze(1).broadcast_to([1, 32, H]), ALU.is_ge))
                ch.link(dve.tensor_reduce(head_f[:, :], headcmp[:, :, :], AX.X, ALU.add))
                ch.done(dve.tensor_scalar(head_i[:, :], head_f[:, :], -1.0, None, ALU.add))
                ch.link(dve.scalar_tensor_tensor(
                    out=small[:, 3], in0=nh[:, 2].unsqueeze(1).broadcast_to([P, NT, H]), scalar=float(P),
                    in1=rank_ps.rearrange("p (n h) -> p n h", h=H), op0=ALU.mult, op1=ALU.add))
                for j in range(TOPK):
                    ch.link(dve.scalar_tensor_tensor(out=small[:, 4], in0=small[:, 2], scalar=float(j),
                                                     in1=small[:, 1], op0=ALU.is_equal, op1=ALU.mult))
                    ch.done(dve.tensor_tensor(small[:, 5], small[:, 4], small[:, 3], ALU.mult))
                    ch.link(dve.scalar_tensor_tensor(out=small[:, 6], in0=small[:, 4], scalar=0.5,
                                                     in1=sg[:, :, :], op0=ALU.mult, op1=ALU.mult))
                    ch.done(dve.tensor_reduce(slot_f[:, j, :], small[:, 5], AX.X, ALU.add))
                    ch.link(dve.tensor_reduce(gate[:, j, :], small[:, 6], AX.X, ALU.add))
                dve.tensor_copy(slot_i[:, :, :], slot_f[:, :, :]).then_inc(slots_made, 1)
                assert ch.n == GATE_CHAIN, ch.n

            def keys_lo(f):
                for h in range(H):
                    dve.wait_ge(a_hi_made, f * H + (h + 1))
                    dve.tensor_tensor(A_lo[:, h * T:(h + 1) * T], S[:, h % 2, :],
                                      A_hi[:, h * T:(h + 1) * T].bitcast(F32), ALU.subtract).then_inc(a_lo_made, 1)

            def s_max(f, t, par):
                dve.wait_ge(s_made, f * NS + t + 1)
                dve.tensor_reduce(mx[:, par:par + 1], S[:, par, :], AX.X, ALU.max, negate=True).then_inc(max_made, 1)

            def pT_copy(f, t, par):
                dve.wait_ge(p_turned, (f * NS + t) * 2 + 2)
                if not isinstance(t, int) or t >= 2:
                    dve.wait_ge(o_made, f * NS + t - 1)
                dve.tensor_copy(probsT[:, par, 512:1024], TP[:, 512:1024]).then_inc(pT_b, 1)

            def x_lo(f, t, par):
                dve.wait_ge(xs_hi_made, f * NS + t + 1)
                dve.tensor_tensor(xs_lo[:, par, :], xT_ps, xs_hi[:, par, :].bitcast(F32),
                                  ALU.subtract).then_inc(xs_lo_made, 1)

            def o_norm(f, t, par):
                dve.wait_ge(p_made, f * NS + t + 1)
                dve.reciprocal(rden[:, par:par + 1], den[:, bass.ds(t, 1)]).then_inc(rden_made, 1)
                dve.wait_ge(rden_made, f * NS + t + 1)
                dve.wait_ge(o_made, f * NS + t + 1)
                if not isinstance(t, int) or t >= 2:
                    dve.wait_ge(o_turned, f * NS + t - 1)
                dve.tensor_scalar(o_sb[:, par, :], OB[:, par * DH:(par + 1) * DH], rden[:, par:par + 1], None,
                                  ALU.mult).then_inc(o_normed, 1)

            def step(f, s, par, half=None):
                k = 5 if half is not None else s
                live = lambda t: 0 <= t < NS
                if live(k + 1):
                    s_max(f, s + 1, 1 - par)
                if live(k):
                    pT_copy(f, s, par)
                if live(k + 2):
                    x_lo(f, s + 2, par)
                if live(k - 2):
                    dve.wait_ge(y_made, f * NS + (s - 1))
                    if half is not None or s - 2 >= 2:
                        n = half + 1 if half is not None else (s - 2) // 2
                        dve.wait_ge(y_stored[par], (f * (16 - par) + n) * 16)
                    dve.tensor_copy(y_sb[:, par, :], y_ps).then_inc(y_copied, 1)
                if live(k - 1):
                    o_norm(f, s - 1, 1 - par)

            def ffn(layer):
                with dve.Fori(0, NB) as b:
                    f = b + layer * NB
                    norm(b, f + layer * NB)
                    gates(f)
                    keys_lo(f)
                    for s in range(-2, 4):
                        step(f, s, s % 2)
                    with dve.Fori(0, 12) as i:
                        for par in range(2):
                            step(f, i * 2 + (4 + par), par, half=i)
                    for s in range(28, NS + 2):
                        step(f, s, s % 2)
                    dve.wait_ge(y_gathered, (f + 1) * (TOPK * NT * 16))
                    for j in range(TOPK):
                        for n in range(NT):
                            tok = x[:, bass.ds(b * T + n * C, C)]
                            ins = dve.scalar_tensor_tensor(out=tok, in0=y_got[:, j, n, :], scalar=gate[:, j, n:n + 1],
                                                           in1=tok, op0=ALU.mult, op1=ALU.add)
                        if j < TOPK - 1:
                            ins.then_inc(add_chain, 1)
                            dve.wait_ge(add_chain, f * (TOPK - 1) + (j + 1))
                    ins.then_inc(ffn_done, 1)
                    dve.wait_ge(ffn_done, f + 1)

            def time_mix(b):
                r = b + NB
                norm(b, r)
                ch = Chain(dve, wkv_chain, b * WKV_CHAIN)
                now, last = xT[:, 1:1 + T], xT[:, 0:T]
                dve.wait_ge(xT_made, r + 1)
                ch.link(dve.tensor_tensor(area(0), now, last, ALU.subtract))
                for i in range(3):
                    dve.scalar_tensor_tensor(out=area(1 + i), in0=area(0), scalar=cols[:, 2 + i:3 + i], in1=last,
                                             op0=ALU.mult, op1=ALU.add).then_inc(mixed, 1)
                k, v = area(4), area(5)
                pp, aa, bb = area(0, T + 1), area(8, T + 1), area(9, T + 1)
                p_new, p_old = pp[:, 1:1 + T], pp[:, 0:T]
                dve.wait_ge(kvr_copied, b * 3 + 3)
                dve.wait_ge(mixed, b * 3 + 3)
                dve.memset(pp[:, 0:1], NEG_INF)
                dve.memset(aa[:, 0:1], 0.0)
                ch.link(dve.memset(bb[:, 0:1], 0.0))
                ch.link(dve.tensor_tensor_scan(p_new, w_rows[:, :], k, NEG_INF, ALU.add, ALU.max))
                w, u = cols[:, 5:6], cols[:, 1:2]
                dve.scalar_tensor_tensor(out=area(1), in0=p_old, scalar=w, in1=p_new,
                                         op0=ALU.add, op1=ALU.subtract).then_inc(arg_made, 1)
                dve.tensor_tensor(area(2), k, p_new, ALU.subtract).then_inc(arg_made, 1)
                ch.link(dve.scalar_tensor_tensor(out=area(10), in0=k, scalar=u, in1=p_old, op0=ALU.add, op1=ALU.max))
                dve.tensor_tensor(area(3), p_old, area(10), ALU.subtract).then_inc(arg_made, 1)
                dve.scalar_tensor_tensor(out=area(7), in0=k, scalar=u, in1=area(10),
                                         op0=ALU.add, op1=ALU.subtract).then_inc(arg_made, 1)
                dve.wait_ge(exp_made, b * 4 + 2)
                dve.wait_ge(arg_made, b * 4 + 4)
                ch.done(dve.tensor_tensor_scan(bb[:, 1:1 + T], area(1), area(2), 0.0, ALU.mult, ALU.add))
                ch.link(dve.tensor_tensor(area(10), area(2), v, ALU.mult))
                ch.link(dve.tensor_tensor_scan(aa[:, 1:1 + T], area(1), area(10), 0.0, ALU.mult, ALU.add))
                dve.wait_ge(exp_made, b * 4 + 4)
                ch.done(dve.tensor_tensor(area(1), area(3), aa[:, 0:T], ALU.mult))
                ch.done(dve.tensor_tensor(area(2), area(7), v, ALU.mult))
                ch.link(dve.tensor_tensor(area(10), area(3), bb[:, 0:T], ALU.mult))
                ch.done(dve.tensor_tensor(area(1), area(1), area(2), ALU.add))
                ch.link(dve.tensor_tensor(area(10), area(10), area(7), ALU.add))
                ch.link(dve.scalar_tensor_tensor(out=area(10), in0=area(6), scalar=1.0, in1=area(10),
                                                 op0=ALU.add, op1=ALU.mult))
                ch.link(dve.reciprocal(area(10), area(10)))
                dve.tensor_tensor(area(2), area(1), area(10), ALU.mult).then_inc(rw_made, 1)
                dve.wait_ge(ro_made, b + 1)
                xb = x[:, bass.ds(b * T, T)]
                ch.link(dve.tensor_tensor(xb, TP[:, :], xb, ALU.add))
                assert ch.n == WKV_CHAIN, ch.n

            dve.wait_ge(cols_made, 4)
            dve.wait_ge(loaded, 16 * NLOAD)
            ffn(0)
            with dve.Fori(0, NB) as b:
                time_mix(b)
            ffn(1)

        @block.tensor
        def _(pe):
            pe.wait_ge(loaded, 16 * NLOAD)
            pe.wait_ge(consts, NCONST)
            for i, w in enumerate((wq_raw, wk_raw)):
                for h in range(H):
                    pe.transpose(S[0:DH, i, h * C:(h + 1) * C], w[:, h * DH:(h + 1) * DH], ident[:, :])
            for i in range(4):
                ins = pe.transpose(TP[:, i * C:(i + 1) * C], rw_raw[:, i, :], ident[:, :])
            ins.then_inc(w_turned, 1)
            pe.wait_ge(w_copied, 2)
            pe.wait_ge(rw_copied, 1)
            for h in range(H):
                ins = pe.matmul(S[:, 0, h * C:(h + 1) * C], wkT[:, h, :], wqT[:, h, :], start=True, stop=True)
            ins.then_inc(g_made, 1)
            pe.wait_ge(g_copied, 1)

            def turn(r):
                pe.wait_ge(xn_made, r + 1)
                for n in range(NT):
                    ins = pe.transpose(S[:, 0, n * P:(n + 1) * P], xn[:, n * C:(n + 1) * C], ident[:, :])
                ins.then_inc(xn_turned, 1)
                pe.wait_ge(xT_made, r + 1)

            def xT_tile(n):
                return xT[:, 1 + n * P:1 + (n + 1) * P]

            def gates(f):
                for n in range(NT):
                    ins = pe.matmul(logit_ps[:, n * H:(n + 1) * H], xT_tile(n), ws[:, :], start=True, stop=True)
                ins.then_inc(logits_made, 1)

            def ranks(f):
                pe.wait_ge(mask_made, f + 1)
                m = mask_b[:, :, :].rearrange("p n h -> p (n h)")
                pe.matmul(rank_ps, tri[:, :], m, start=True, stop=False, skip_group_check=True)
                for d in range(1, NT):
                    pe.matmul(rank_ps[:, d * H:NT * H], ones[:, :], m[:, 0:(NT - d) * H], start=False,
                              stop=(d == NT - 1), skip_group_check=True)
                for n in range(NT):
                    ins = pe.matmul(count_ps, ones[:, :], mask_b[:, n, :], start=(n == 0), stop=(n == NT - 1))
                ins.then_inc(rank_made, 1)

            def keys_values(f):
                for h in range(H):
                    if h >= 2:
                        pe.wait_ge(a_lo_made, f * H + (h - 1))
                    for i in range(2):
                        ins = pe.matmul(S[:, h % 2, i * 512:(i + 1) * 512], GT[:, h, :],
                                        xT[:, 1 + i * 512:1 + (i + 1) * 512], start=True, stop=True)
                    ins.then_inc(a_made, 1)
                for n in range(NT):
                    if n >= 2:
                        pe.wait_ge(v_copied, f * NT + (n - 1))
                    pe.matmul(TP[:, (n % 2) * 512:(n % 2) * 512 + 512], xT_tile(n), wv[:, :],
                              start=True, stop=True).then_inc(v_made, 1)
                pe.wait_ge(a_lo_made, (f + 1) * H)
                pe.wait_ge(v_copied, (f + 1) * NT)

            def turn_slots(f, t, par, n):
                pe.wait_ge(xs_loaded[par], (f * (16 - par) + n + 1) * 16)
                if not isinstance(t, int) or t >= 1:
                    pe.wait_ge(xs_lo_made, f * NS + t)
                pe.transpose(xT_ps, xs[:, par, :], ident[:, :]).then_inc(xs_turned, 1)

            def scores(f, t, par):
                head = pe.value_load(head_i[0:1, bass.ds(t, 1)], min_val=0, max_val=H - 1)
                pe.wait_ge(xs_lo_made, f * NS + t + 1)
                if not isinstance(t, int) or t >= 2:
                    pe.wait_ge(p_made, f * NS + t - 1)
                terms = ((xs_hi, A_hi), (xs_lo, A_hi), (xs_hi, A_lo))
                for n, (xx, A) in enumerate(terms):
                    for i in range(2):
                        ins = pe.matmul(S[:, par, i * 512:(i + 1) * 512], xx[:, par, :],
                                        A[:, bass.ds(head * T + i * 512, 512)], start=(n == 0), stop=(n == 2))
                ins.then_inc(s_made, 1)

            def turn_probs(f, t, par):
                pe.wait_ge(p_made, f * NS + t + 1)
                for i, free in enumerate((pT_a, pT_b)):
                    if not isinstance(t, int) or t >= 1:
                        pe.wait_ge(free, f * NS + t)
                    for n in range(4 * i, 4 * i + 4):
                        ins = pe.transpose(TP[:, n * P:(n + 1) * P], probs[:, par, n * P:(n + 1) * P], ident[:, :])
                    ins.then_inc(p_turned, 1)

            def outputs(f, t, par):
                head = pe.value_load(head_i[0:1, bass.ds(t, 1)], min_val=0, max_val=H - 1)
                pe.wait_ge(pT_a, f * NS + t + 1)
                pe.wait_ge(pT_b, f * NS + t + 1)
                if not isinstance(t, int) or t >= 1:
                    pe.wait_ge(o_normed, f * NS + t)
                for n in range(NT):
                    ins = pe.matmul(OB[:, par * DH:(par + 1) * DH], probsT[:, par, n * P:(n + 1) * P],
                                    V[:, bass.ds(head * DH + n * (H * DH), DH)], start=(n == 0), stop=(n == NT - 1))
                ins.then_inc(o_made, 1)

            def turn_out(f, t, par):
                pe.wait_ge(o_normed, f * NS + t + 1)
                if not isinstance(t, int) or t >= 1:
                    pe.wait_ge(y_copied, f * NS + t)
                if not isinstance(t, int) or t + 3 < NS:
                    pe.wait_ge(xs_lo_made, f * NS + t + 4)
                pe.sem_inc(passed, 1)
                pe.transpose(oT_ps, o_sb[:, par, :], ident[:, :]).then_inc(o_turned, 1)

            def project(f, t, par):
                head = pe.value_load(head_i[0:1, bass.ds(t, 1)], min_val=0, max_val=H - 1)
                pe.wait_ge(oT_copied, f * NS + t + 1)
                pe.matmul(y_ps, oT[:, par, :], wo[:, bass.ds(head * C, C)], start=True, stop=True).then_inc(y_made, 1)

            def step(f, s, par, half=None):
                k = 5 if half is not None else s
                live = lambda t: 0 <= t < NS
                if live(k + 1):
                    scores(f, s + 1, 1 - par)
                if live(k - 2):
                    turn_out(f, s - 2, par)
                if live(k):
                    turn_probs(f, s, par)
                if live(k - 2):
                    project(f, s - 2, par)
                if live(k + 2):
                    turn_slots(f, s + 2, par, half + 3 if half is not None else (s + 2) // 2)
                if live(k - 1):
                    outputs(f, s - 1, 1 - par)

            def ffn(layer):
                with pe.Fori(0, NB) as b:
                    f = b + layer * NB
                    turn(f + layer * NB)
                    gates(f)
                    ranks(f)
                    keys_values(f)
                    pe.wait_ge(slots_made, f + 1)
                    for s in range(-2, 4):
                        step(f, s, s % 2)
                    with pe.Fori(0, 12) as i:
                        for par in range(2):
                            step(f, i * 2 + (4 + par), par, half=i)
                    for s in range(28, NS + 2):
                        step(f, s, s % 2)
                    pe.wait_ge(ffn_done, f + 1)

            ffn(0)
            with pe.Fori(0, NB) as b:
                turn(b + NB)
                for i, dst in enumerate((S[:, 0, :], S[:, 1, :], TP[:, :])):
                    pe.wait_ge(mixed, b * 3 + (i + 1))
                    for c in range(2):
                        ins = pe.matmul(dst[:, c * 512:(c + 1) * 512], rw_T[:, i, :], area(1 + i)[:, c * 512:(c + 1) * 512],
                                        start=True, stop=True)
                    ins.then_inc(kvr_made, 1)
                pe.wait_ge(rw_made, b + 1)
                for n in range(NT):
                    ins = pe.matmul(TP[:, n * C:(n + 1) * C], area(2)[:, n * P:(n + 1) * P], rw_T[:, 3, :],
                                    start=True, stop=True)
                ins.then_inc(ro_made, 1)
                pe.wait_ge(wkv_chain, (b + 1) * WKV_CHAIN)
            ffn(1)


_INS = ['L0_attn_x', 'L0_attn_time_decay', 'L0_attn_time_first', 'L0_attn_time_mix_k', 'L0_attn_time_mix_v',
        'L0_attn_time_mix_r', 'L0_attn_Wk', 'L0_attn_Wv', 'L0_attn_Wr', 'L0_attn_Wo', 'L0_ffn_Wq', 'L0_ffn_Wkv',
        'L0_ffn_Ws', 'L0_ffn_Wo', 'L0_ffn_bo']
_OUTS = [((8, 1024, 128), 'float32')]


def kernel(**inputs):
    import numpy as _np
    import concourse.bacc as _bacc
    from concourse import mybir as _mybir
    from concourse.bass_utils import run_bass_kernel_spmd as _run

    nc = _bacc.Bacc("TRN2", target_bir_lowering=False, num_devices=1)
    arrays, args = {}, []
    for name in _INS:
        a = _np.ascontiguousarray(inputs[name])
        arrays[f"in_{name}_dram"] = a
        args.append(nc.dram_tensor(f"in_{name}_dram", a.shape, _mybir.dt.from_np(a.dtype), kind="ExternalInput").ap())
    for i, (shape, dtype) in enumerate(_OUTS):
        dt = _mybir.dt.from_np(_np.dtype(dtype))
        args.append(nc.dram_tensor(f"out_{i}_dram", shape, dt, kind="ExternalOutput").ap())
    build(nc, *args)
    r = _run(nc, [arrays], core_ids=[0])
    got = tuple(r.results[0][f"out_{i}_dram"] for i in range(len(_OUTS)))
    return got[0]
```

```python
from contextlib import ExitStack

import concourse.bass as bass
from concourse import mybir

F32 = mybir.dt.float32
F32R = mybir.dt.float32r
BF16 = mybir.dt.bfloat16
I32 = mybir.dt.int32
U32 = mybir.dt.uint32
ALU = mybir.AluOpType
ACT = mybir.ActivationFunctionType
AX = mybir.AxisListType

P = 128
NB, T, C = 8, 1024, 128
NT = T // P
H, DH, TOPK = 8, 64, 3
NS = (TOPK * T + H * (P - 1)) // P
SLOTS = NS * P
EPS = 1e-5
NEG_INF = -1e38
SCALE = DH ** -0.5

GATE_CHAIN, WKV_CHAIN = 62, 13

AHEAD, BEHIND = 3, 3
LN_STEP, TURN_STEP, LOGIT_STEP, RANK_STEP = 12, 12, 13, 21


class Chain:

    def __init__(self, eng, sem, start, passed=None):
        self.eng, self.sem, self.start, self.passed, self.n = eng, sem, start, passed, 0

    def done(self, ins):
        self.n += 1
        ins.then_inc(self.sem, 1)

    def wait(self):
        self.eng.wait_ge(self.sem, self.start + self.n)
        if self.passed is not None:
            self.eng.sem_inc(self.passed, 1)

    def link(self, ins):
        self.done(ins)
        self.wait()


class Tile:

    def __init__(self, t, least, half):
        self.t, self.least, self.par, self.same = t, least, least % 2, half

    def live(self):
        return 0 <= self.least < NS


class Step:
    def __init__(self, s, i=None):
        self.s, self.i = s, i

    def tile(self, c):
        t = self.s + c
        if self.i is None:
            return Tile(t, t, t // 2)
        return Tile(self.i * 2 + t, t, self.i + t // 2)


def pipeline(eng, step, between):
    s = -AHEAD
    for stop, looped in ((6, 0), (12, 1), (14, 0), (20, 1), (22, 0), (26, 1), (NS + BEHIND, 0)):
        if looped:
            with eng.Fori(0, (stop - s) // 2) as i:
                for par in range(2):
                    step(Step(s + par, i))
            s = stop
        while s < stop:
            between(s)
            step(Step(s))
            s += 1


def build(nc, x_in, time_decay, time_first, mix_k, mix_v, mix_r, rk_w, rv_w, rr_w, ro_w,
          q_w, kv_w, s_w, o_w, o_b, out):
    ctx = ExitStack()
    with ctx:
        def sb(name, shape, dt=F32):
            return ctx.enter_context(nc.sbuf_tensor(name, shape, dt))

        def sem(name):
            return ctx.enter_context(nc.semaphore(name))

        x_slots = nc.dram_tensor("x_slots", (2 * SLOTS, C), F32, kind="Internal").ap()
        y_slots = nc.dram_tensor("y_slots", (2 * SLOTS, C), F32, kind="Internal").ap()

        x = sb("x", [P, NB * T])
        A_hi = sb("A_hi", [P, H * T], F32R)
        A_lo = sb("A_lo", [P, H * T], F32R)
        V = sb("V", [P, H, NT, 2, DH], F32R)
        xn = sb("xn", [P, NT * C])
        xT = sb("xT", [P, 1 + T])
        pT_hi = sb("pT_hi", [P, 2, T], F32R)
        pT_lo = sb("pT_lo", [P, 2, T], F32R)
        xs_hi = sb("xs_hi", [P, 2, P], F32R)
        xs_lo = sb("xs_lo", [P, 2, P], F32R)
        GT = sb("GT", [P, H, C])
        wv = sb("wv", [P, H * DH])
        wo = sb("wo", [P, H * C])
        bias = sb("bias", [33, H * C], F32R)
        ones33 = sb("ones33", [33, P], F32R)
        ws = sb("ws", [P, H])
        ident = sb("ident", [P, P])
        tri = sb("tri", [P, P], BF16)
        ones = sb("ones", [P, P], BF16)
        lower = sb("lower", [P, H, H])
        steps = sb("steps", [P, H, H])
        tile_no = sb("tile_no", [1, 32])
        rw_T = sb("rw_T", [P, 4, C])
        cols = sb("cols", [P, 6])
        mx = sb("mx", [P, 2])
        den = sb("den", [P, NS + 1])
        rden = sb("rden", [P, 2])
        stats = sb("stats", [P, NT, 6])
        mv = sb("mv", [P, NT, 2])
        rstd = sb("rstd", [P, 2, NT])
        powr = sb("powr", [P, NT])
        mask_b = sb("mask_b", [P, NT, H], BF16)
        ranks_sb = sb("ranks_sb", [P, NT * H + H])
        nh = sb("nh", [P, 4, H])
        flip = sb("flip", [P, 1])
        slot_f = sb("slot_f", [P, TOPK, NT])
        slot_next = sb("slot_next", [P, TOPK, NT], U32)
        slot_now = sb("slot_now", [P, TOPK, NT], U32)
        gate_next = sb("gate_next", [P, TOPK, NT])
        gate_now = sb("gate_now", [P, TOPK, NT])
        head_next = sb("head_next", [1, 32], I32)
        head_of = sb("head_of", [1, 2 * 32], I32)

        work = sb("work", [P, 8 * (T + 2)])
        at = 0

        def take(*shape):
            nonlocal at
            n = 1
            for d in shape:
                n *= d
            names = "abc"[:len(shape)]
            v = work[:, at:at + n]
            at += n
            if len(shape) > 1:
                v = v.rearrange(f"p ({' '.join(names)}) -> p {' '.join(names)}", **dict(zip(names, shape)))
            return v

        probs = take(2, T)
        y_got = take(TOPK, NT, C)
        cmp1 = take(NT, H, H)
        cmp2 = take(NT, H, H)
        small = take(8, NT * H)
        o_sb = take(2, 2 * DH)
        oT = take(2, P)
        xs = take(2, C)
        y_sb = take(2, C)
        eg = take(NT * H)
        sg = take(NT, H)
        assert at <= work.shape[1]
        at = 0
        wq_raw, wk_raw = take(512), take(512)
        wqT, wkT = take(H, C)[0:DH], take(H, C)[0:DH]
        zeros = take(NS * C)
        rw_raw = take(4, C)
        ones_f, ones_h, iota_f = take(P), take(H, H), take(32 * H // 4 * 4)
        iota_i = iota_f.bitcast(I32)

        assert at <= work.shape[1]

        def area(i, n=T):
            return work[:, i * (T + 2):i * (T + 2) + n]

        S = ctx.enter_context(nc.psum_tensor("S", [P, 2, T], F32))
        TP = ctx.enter_context(nc.psum_tensor("TP", [P, T], F32))
        OB = ctx.enter_context(nc.psum_tensor("OB", [P, 512], F32))
        MB = ctx.enter_context(nc.psum_tensor("MB", [P, 512], F32))
        xT_ps, oT_ps, y_ps = MB[:, 0:128], MB[:, 128:256], MB[:, 256:384]
        logit_ps, rank_ps, count_ps = MB[:, 384:448], MB[:, 384:448], MB[:, 448:456]
        o_ps = OB[:, 0:2 * DH]

        loaded, zeroed, consts, pool_setup = sem("loaded"), sem("zeroed"), sem("consts"), sem("pool_setup")
        w_turned, w_copied = sem("w_turned"), sem("w_copied")
        g_made, g_copied = sem("g_made"), sem("g_copied")
        cols_made, bias_made = sem("cols_made"), sem("bias_made")
        stats_made, mv_made, rstd_made, xn_made = sem("stats_made"), sem("mv_made"), sem("rstd_made"), sem("xn_made")
        xn_turned, xT_made = sem("xn_turned"), sem("xT_made")
        logits_made, eg_made, eg1_made, sg_made = sem("logits_made"), sem("eg_made"), sem("eg1_made"), sem("sg_made")
        mask_made, rank_made, rank_copied = sem("mask_made"), sem("rank_made"), sem("rank_copied")
        slots_made, scattered = sem("slots_made"), sem("scattered")
        a_made, a_hi_made, a_lo_made = sem("a_made"), sem("a_hi_made"), sem("a_lo_made")
        v_made, v_hi_made, v_lo_made = sem("v_made"), sem("v_hi_made"), sem("v_lo_made")
        xs_loaded = [sem(f"xs_loaded{i}") for i in range(2)]
        xs_turned, xs_hi_made, xs_lo_made = sem("xs_turned"), sem("xs_hi_made"), sem("xs_lo_made")
        s_made, max_made, p_made = sem("s_made"), sem("max_made"), sem("p_made")
        p_turned, pT_hi_made, pT_lo_made = sem("p_turned"), sem("pT_hi_made"), sem("pT_lo_made")
        o_made, rden_made, o_normed = sem("o_made"), sem("rden_made"), sem("o_normed")
        o_turned, oT_copied, y_made, y_copied = sem("o_turned"), sem("oT_copied"), sem("y_made"), sem("y_copied")
        y_stored = [sem(f"y_stored{i}") for i in range(2)]
        y_gathered, ffn_done = sem("y_gathered"), sem("ffn_done")
        mixed, kvr_made, kvr_copied = sem("mixed"), sem("kvr_made"), sem("kvr_copied")
        arg_made, exp_made, rw_made, ro_made, wkv_done = (sem("arg_made"), sem("exp_made"), sem("rw_made"),
                                                          sem("ro_made"), sem("wkv_done"))
        gate_chain, wkv_chain, add_chain, pow_chain = (sem("gate_chain"), sem("wkv_chain"), sem("add_chain"),
                                                       sem("pow_chain"))
        stored = sem("stored")
        passed = sem("passed")

        NCONST = 14
        NLOAD = NB + 7 + 4 + 5
        NDMA = TOPK * NT * 16
        COMBINE = 6

        block = ctx.enter_context(nc.Block())

        def runs(eng, layer, run):
            with eng.Fori(0, NB - 1) as b:
                run(b, b + layer * NB, True)
            run(NB - 1, NB - 1 + layer * NB, False)

        @block.sync
        def _(sp):
            for b in range(NB):
                sp.dma_start(x[:, b * T:(b + 1) * T].rearrange("p (n c) -> p n c", c=C),
                             x_in[b].rearrange("(n p) c -> p n c", p=P)).then_inc(loaded, 16)
            sp.dma_start(wq_raw, q_w).then_inc(loaded, 16)
            sp.dma_start(wk_raw, kv_w[:, 0:512]).then_inc(loaded, 16)
            sp.dma_start(wv[:, :], kv_w[:, 512:1024]).then_inc(loaded, 16)
            sp.dma_start(ws[:, :], s_w).then_inc(loaded, 16)
            for i in range(2):
                sp.dma_start(wo[i * DH:(i + 1) * DH, :].rearrange("d (h e) -> d h e", h=H),
                             o_w.rearrange("h d e -> d h e")).then_inc(loaded, 16)
            sp.dma_start(xT[0:1, 1:1 + T], o_b.rearrange("(o h) e -> o (h e)", o=1)).then_inc(loaded, 16)
            for i, w in enumerate((rk_w, rv_w, rr_w, ro_w)):
                sp.dma_start(rw_raw[:, i, :], w).then_inc(loaded, 16)
            for i, v in enumerate((time_decay, time_first)):
                sp.dma_start(cols[:, i:i + 1], v.rearrange("(c o) -> c o", o=1)).then_inc(loaded, 16)
            for i, v in enumerate((mix_k, mix_v, mix_r)):
                sp.dma_start(cols[:, 2 + i:3 + i], v.rearrange("a b c -> c (a b)")).then_inc(loaded, 16)
            sp.wait_ge(pool_setup, 1)
            for half in (x_slots[0:SLOTS], x_slots[SLOTS:2 * SLOTS], y_slots[SLOTS:2 * SLOTS]):
                sp.dma_start(half.rearrange("(n p) c -> p n c", p=P),
                             zeros.rearrange("p (n c) -> p n c", c=C)).then_inc(zeroed, 16)

            def run(b, f, _):
                first = (b % 2) * SLOTS
                sp.wait_ge(scattered, (f + 1) * NDMA)

                def step(st):
                    a = st.tile(AHEAD + 1)
                    if a.live():
                        if a.least >= 2:
                            sp.wait_ge(xs_turned, f * NS + a.t - 1)
                        sp.dma_start(xs[:, a.par, :], x_slots[bass.ds(first + a.t * P, P), :]).then_inc(xs_loaded[a.par], 16)
                    y = st.tile(-BEHIND)
                    if y.live():
                        sp.wait_ge(y_copied, f * NS + y.t + 1)
                        sp.dma_start(y_slots[bass.ds(first + y.t * P, P), :], y_sb[:, y.par, :]).then_inc(y_stored[y.par], 16)

                step(Step(-AHEAD - 1))
                pipeline(sp, step, lambda s: None)

            runs(sp, 0, run)
            runs(sp, 1, run)
            sp.wait_ge(ffn_done, 2 * NB)
            for b in range(NB):
                sp.dma_start(out[b].rearrange("(n p) c -> p n c", p=P),
                             x[:, b * T:(b + 1) * T].rearrange("p (n c) -> p n c", c=C)).then_inc(stored, 16)
            sp.wait_ge(stored, 16 * NB)

        @block.gpsimd
        def _(pool):
            pool.memset(zeros, 0.0).then_inc(pool_setup, 1)
            pool.memset(ones_f, 1.0).then_inc(consts, 1)
            pool.memset(ones[:, :], 1.0).then_inc(consts, 1)
            pool.memset(powr[:, :], -0.5).then_inc(consts, 1)
            pool.memset(xT[:, 0:1], 0.0).then_inc(consts, 1)
            pool.memset(ones_h, 1.0).then_inc(consts, 1)
            pool.memset(flip[:, :], float(SLOTS)).then_inc(consts, 1)
            pool.wait_ge(consts, 7)
            pool.affine_select(out=ident[:, :], in_=ones_f, compare_op=ALU.is_equal, fill=0.0, base=0,
                               pattern=[[-1, P]], channel_multiplier=1).then_inc(consts, 1)
            pool.affine_select(out=tri[:, :], in_=ones[:, :], compare_op=ALU.is_gt, fill=0.0, base=0,
                               pattern=[[1, P]], channel_multiplier=-1).then_inc(consts, 1)
            pool.affine_select(out=lower[:, :, :], in_=ones_h, compare_op=ALU.is_gt, fill=0.0, base=0,
                               pattern=[[1, H], [-1, H]], channel_multiplier=0).then_inc(consts, 1)
            pool.iota(iota_i[:, 0:H * H], [[0, H], [P, H]], base=0, channel_multiplier=0).then_inc(consts, 1)
            pool.iota(iota_i[:, H * H:H * H + 32], [[1, 32]], base=0, channel_multiplier=0).then_inc(consts, 1)
            pool.wait_ge(consts, 12)
            pool.tensor_copy(steps[:, :, :].rearrange("p a b -> p (a b)"), iota_i[:, 0:H * H]).then_inc(consts, 1)
            pool.tensor_copy(tile_no[:, :], iota_i[0:1, H * H:H * H + 32]).then_inc(consts, 1)

            def root(r):
                pool.wait_ge(mv_made, r + 1)
                pool.sem_inc(passed, 1)
                pool.tensor_scalar(rstd[:, 0, :], mv[:, :, 1], EPS, None, ALU.add).then_inc(pow_chain, 1)
                pool.wait_ge(pow_chain, r + 1)
                pool.tensor_tensor(rstd[:, 1, :], rstd[:, 0, :], powr[:, :], ALU.pow).then_inc(rstd_made, 1)

            def gates(b, f):
                ch = Chain(pool, gate_chain, f * GATE_CHAIN, passed)
                low = lower[:, :, :].unsqueeze(1).broadcast_to([P, NT, H, H])

                def total(src, tmp, dst):
                    ch.link(pool.tensor_tensor(tmp[..., 0:4], src[..., 0:4], src[..., 4:8], ALU.add))
                    ch.link(pool.tensor_tensor(tmp[..., 0:2], tmp[..., 0:2], tmp[..., 2:4], ALU.add))
                    ch.link(pool.tensor_tensor(dst, tmp[..., 0:1], tmp[..., 1:2], ALU.add))

                def by_head(i):
                    return small[:, i, :].rearrange("p (n h) -> p n h", h=H)

                c1 = cmp1
                c2 = cmp2
                before, mask, chosen_before, slot, sel, pick, weight, tmp8 = (by_head(i) for i in range(8))
                not_chosen, half = sel, before
                pool.wait_ge(sg_made, f + 1)
                pool.sem_inc(passed, 1)
                g_of = sg.unsqueeze(2).broadcast_to([P, NT, H, H])
                h_of = sg.unsqueeze(3).broadcast_to([P, NT, H, H])
                ch.link(pool.tensor_tensor(c1, g_of, h_of, ALU.subtract))
                ch.link(pool.tensor_scalar(c2, c1, 0.0, None, ALU.is_equal))
                ch.link(pool.tensor_tensor(c2, c2, low, ALU.mult))
                ch.link(pool.tensor_scalar(c1, c1, 0.0, None, ALU.is_gt))
                ch.link(pool.tensor_tensor(c1, c1, c2, ALU.add))
                total(c1, c2, before.unsqueeze(3))
                ch.link(pool.tensor_scalar(mask, before, float(TOPK), None, ALU.is_lt))
                pool.tensor_copy(mask_b[:, :, :], mask).then_inc(mask_made, 1)
                ch.link(pool.tensor_tensor(c1, mask.unsqueeze(2).broadcast_to([P, NT, H, H]), low, ALU.mult))
                total(c1, c2, chosen_before.unsqueeze(3))
                ch.link(pool.tensor_scalar(not_chosen, mask, -float(H), float(H), ALU.mult, ALU.add))
                ch.link(pool.tensor_tensor(chosen_before, chosen_before, not_chosen, ALU.add))
                ch.link(pool.tensor_scalar(half, sg, 0.5, None, ALU.mult))
                pool.wait_ge(rank_copied, f + 1)
                pool.sem_inc(passed, 1)
                count = ranks_sb[:, NT * H:].unsqueeze(2).broadcast_to([P, H, H])
                m1, m2 = c1[:, 0], c2[:, 0]
                tiles, first_tile = nh[:, 0], nh[:, 1]
                ch.link(pool.tensor_tensor(m1, count, steps[:, :, :], ALU.subtract))
                ch.link(pool.tensor_scalar(m1, m1, 0.0, None, ALU.is_gt))
                total(m1, m2, tiles.unsqueeze(2))
                ch.link(pool.tensor_tensor(m1, tiles.unsqueeze(1).broadcast_to([P, H, H]), lower[:, :, :], ALU.mult))
                total(m1, m2, first_tile.unsqueeze(2))
                t1 = c1[0:1, 0:4].rearrange("p a b c -> p (a b) c")
                t2 = c2[0:1, 0:4].rearrange("p a b c -> p (a b) c")
                t3 = c2[0:1, 4, 0:4].rearrange("p a b -> p (a b)").unsqueeze(2)
                ch.link(pool.tensor_tensor(t1, tile_no[:, :].unsqueeze(2).broadcast_to([1, 32, H]),
                                           first_tile[0:1].unsqueeze(1).broadcast_to([1, 32, H]), ALU.subtract))
                ch.link(pool.tensor_scalar(t1, t1, 0.0, None, ALU.is_ge))
                total(t1, t2, t3)
                ch.link(pool.tensor_scalar(head_next[:, :].unsqueeze(2), t3, -1.0, None, ALU.add))
                ch.done(pool.tensor_copy(head_of[:, bass.ds((b % 2) * 32, 32)], head_next[:, :]))
                ch.link(pool.tensor_scalar(flip[:, :], flip[:, :], -1.0, float(SLOTS), ALU.mult, ALU.add))
                ch.link(pool.tensor_scalar(first_tile, first_tile, float(P), None, ALU.mult))
                ch.link(pool.tensor_tensor(slot, first_tile.unsqueeze(1).broadcast_to([P, NT, H]),
                                           ranks_sb[:, 0:NT * H].rearrange("p (n h) -> p n h", h=H), ALU.add))
                for j in range(TOPK):
                    ch.link(pool.tensor_scalar(sel, chosen_before, float(j), None, ALU.is_equal))
                    ch.done(pool.tensor_tensor(pick, sel, slot, ALU.mult))
                    ch.link(pool.tensor_tensor(weight, sel, half, ALU.mult))
                    total(pick, tmp8, slot_f[:, j, :].unsqueeze(2))
                    total(weight, tmp8, gate_next[:, j, :].unsqueeze(2))
                assert ch.n == GATE_CHAIN, ch.n
                pool.tensor_scalar(slot_next[:, :, :], slot_f[:, :, :], flip[:, 0:1], None, ALU.add).then_inc(slots_made, 1)

            def prepare(b, f, r):
                root(r)
                gates(b, f)
                pool.wait_ge(slots_made, f + 1)
                pool.sem_inc(passed, 1)
                for j in range(TOPK):
                    for n in range(NT):
                        pool.indirect_dma_start(
                            out=x_slots, out_offset=bass.IndirectOffsetOnAxis(ap=slot_next[:, j, n:n + 1], axis=0),
                            in_=xn[:, n * C:(n + 1) * C], in_offset=None).then_inc(scattered, 16)

            def turn_over(f):
                ch = Chain(pool, add_chain, f * COMBINE)
                ch.done(pool.tensor_copy(slot_now[:, :, :], slot_next[:, :, :]))
                ch.link(pool.tensor_copy(gate_now[:, :, :], gate_next[:, :, :]))

            def combine(b, f):
                pool.wait_ge(y_stored[0], (f + 1) * (16 * 16))
                pool.wait_ge(y_stored[1], (f + 1) * (15 * 16))
                pool.sem_inc(passed, 1)
                for j in range(TOPK):
                    for n in range(NT):
                        pool.indirect_dma_start(
                            out=y_got[:, j, n, :], out_offset=None, in_=y_slots,
                            in_offset=bass.IndirectOffsetOnAxis(ap=slot_now[:, j, n:n + 1], axis=0)).then_inc(y_gathered, 16)
                ch = Chain(pool, add_chain, f * COMBINE + 2)
                pool.wait_ge(y_gathered, (f + 1) * NDMA)
                g = gate_now[:, :, :].rearrange("p j n -> p (j n)").unsqueeze(2).broadcast_to([P, TOPK * NT, C])
                yy = work[:, 2 * T:5 * T].rearrange("p (m c) -> p m c", c=C)
                ch.link(pool.tensor_tensor(yy, yy, g, ALU.mult))
                y0, y1, y2 = (work[:, (2 + j) * T:(3 + j) * T] for j in range(TOPK))
                ch.link(pool.tensor_tensor(y0, y0, y1, ALU.add))
                ch.link(pool.tensor_tensor(y0, y0, y2, ALU.add))
                xb = x[:, bass.ds(b * T, T)]
                ch.link(pool.tensor_tensor(xb, xb, y0, ALU.add))
                assert ch.n == COMBINE - 2
                pool.sem_inc(ffn_done, 1)

            def ffn(layer):
                f0 = layer * NB
                prepare(0, f0, 2 * layer * NB)
                turn_over(f0)

                def run(b, f, more):
                    if more:
                        prepare(b + 1, f + 1, f + (layer * NB + 1))
                    combine(b, f)
                    if more:
                        turn_over(f + 1)

                runs(pool, layer, run)

            pool.wait_ge(zeroed, 48)
            ffn(0)
            with pool.Fori(0, NB) as b:
                root(b + NB)
            ffn(1)

        @block.scalar
        def _(act):
            act.wait_ge(w_turned, 1)
            act.activation(wqT.rearrange("p h c -> p (h c)"), S[0:DH, 0, :], ACT.Copy).then_inc(w_copied, 1)
            act.activation(wkT.rearrange("p h c -> p (h c)"), S[0:DH, 1, :], ACT.Copy).then_inc(w_copied, 1)
            act.activation(rw_T[:, :, :].rearrange("p a b -> p (a b)"), TP[:, 0:512], ACT.Copy).then_inc(w_copied, 1)
            act.wait_ge(g_made, 1)
            act.activation(GT[:, :, :].rearrange("p h c -> p (h c)"), S[:, 0, :], ACT.Copy, scale=SCALE).then_inc(g_copied, 1)
            act.wait_ge(loaded, 16 * NLOAD)
            act.activation(cols[:, 5:6], cols[:, 0:1], ACT.Exp).then_inc(cols_made, 1)
            act.wait_ge(bias_made, 1)
            act.activation(bias[0:1, :], xT[0:1, 1:1 + T], ACT.Copy).then_inc(bias_made, 1)

            def transpose_out(r):
                act.wait_ge(xn_turned, r + 1)
                act.activation(xT[:, 1:1 + T], TP[:, :], ACT.Copy).then_inc(xT_made, 1)

            def gate_exp(f):
                act.wait_ge(logits_made, f + 1)
                act.activation(eg, logit_ps, ACT.Exp, scale=-1.0).then_inc(eg_made, 1)

            def rank_copy(f):
                act.wait_ge(rank_made, f + 1)
                act.activation(ranks_sb[:, :], MB[:, 384:456], ACT.Copy).then_inc(rank_copied, 1)

            def keys_values(f):
                for h in range(H):
                    act.wait_ge(a_made, f * H + (h + 1))
                    act.activation(A_hi[:, h * T:(h + 1) * T], S[:, h % 2, :], ACT.Copy).then_inc(a_hi_made, 1)
                for n in range(NT):
                    act.wait_ge(v_made, f * NT + (n + 1))
                    act.activation(V[:, :, n, 0, :], TP[:, (n % 2) * 512:(n % 2) * 512 + 512].rearrange("p (h d) -> p h d", h=H),
                                   ACT.Copy).then_inc(v_hi_made, 1)

            def run(layer, b, f, more):
                keys_values(f)

                def step(st):
                    y = st.tile(-BEHIND)
                    if y.live():
                        act.wait_ge(o_turned, f * NS + y.t + 1)
                        act.activation(oT[:, y.par, :], oT_ps, ACT.Copy).then_inc(oT_copied, 1)
                    p = st.tile(0)
                    if p.live():
                        for i in range(2):
                            act.wait_ge(p_turned, (f * NS + p.t) * 2 + (i + 1))
                            if p.least >= 2:
                                act.wait_ge(o_made, f * NS + p.t - 1)
                            act.activation(pT_hi[:, p.par, i * 512:(i + 1) * 512], TP[:, i * 512:(i + 1) * 512],
                                           ACT.Copy).then_inc(pT_hi_made, 1)
                    if y.live():
                        act.wait_ge(y_made, f * NS + y.t + 1)
                        a = st.tile(AHEAD)
                        if a.live():
                            act.wait_ge(xs_turned, f * NS + a.t + 1)
                        if more and st.s == LOGIT_STEP:
                            gate_exp(f + 1)
                        if more and st.s == RANK_STEP:
                            rank_copy(f + 1)
                        if y.least >= 2:
                            act.wait_ge(y_stored[y.par], (f * (16 - y.par) + y.same) * 16)
                        act.activation(y_sb[:, y.par, :], y_ps, ACT.Copy).then_inc(y_copied, 1)
                    a = st.tile(AHEAD)
                    if a.live():
                        act.wait_ge(xs_turned, f * NS + a.t + 1)
                        if a.least >= 2:
                            act.wait_ge(s_made, f * NS + a.t - 1)
                        act.activation(xs_hi[:, a.par, :], xT_ps, ACT.Copy).then_inc(xs_hi_made, 1)
                    e = st.tile(1)
                    if e.live():
                        act.wait_ge(max_made, f * NS + e.t + 1)
                        if e.least >= 2:
                            act.wait_ge(p_turned, (f * NS + e.t) * 2 - 2)
                        act.activation(probs[:, e.par, :], S[:, e.par, :], ACT.Exp, bias=mx[:, e.par:e.par + 1],
                                       accum_out=den[:, bass.ds(e.t, 1)]).then_inc(p_made, 1)
                    if more and st.s == TURN_STEP:
                        transpose_out(f + (layer * NB + 1))

                pipeline(act, step, lambda s: None)

            def ffn(layer):
                f0 = layer * NB
                transpose_out(2 * layer * NB)
                gate_exp(f0)
                rank_copy(f0)
                runs(act, layer, lambda b, f, more: run(layer, b, f, more))

            ffn(0)
            with act.Fori(0, NB) as b:
                transpose_out(b + NB)
                for i, (dst, src) in enumerate(((area(4), S[:, 0, :]), (area(5), S[:, 1, :]))):
                    act.wait_ge(kvr_made, b * 3 + (i + 1))
                    act.activation(dst, src, ACT.Copy).then_inc(kvr_copied, 1)
                act.wait_ge(kvr_made, b * 3 + 3)
                act.activation(xT[:, 1:1 + T], TP[:, :], ACT.Exp, scale=-1.0).then_inc(kvr_copied, 1)
                for i, a in enumerate((1, 2, 3, 6)):
                    act.wait_ge(arg_made, b * 4 + (i + 1))
                    act.activation(area(a), area(a), ACT.Exp).then_inc(exp_made, 1)
            ffn(1)

        @block.vector
        def _(dve):
            dve.memset(ones33[:, :].bitcast(F32), 1.0).then_inc(consts, 1)
            dve.memset(bias[:, :].bitcast(F32), 0.0).then_inc(bias_made, 1)
            dve.wait_ge(cols_made, 1)
            dve.wait_ge(consts, NCONST)
            dve.tensor_scalar(cols[:, 5:6], cols[:, 5:6], -1.0, None, ALU.mult).then_inc(cols_made, 1)
            dve.wait_ge(cols_made, 2)
            dve.wait_ge(bias_made, 2)
            dve.tensor_tensor(bias[32:33, :], xT[0:1, 1:1 + T], bias[0:1, :].bitcast(F32), ALU.subtract).then_inc(bias_made, 1)

            def norm_stats(b, r):
                for n in range(NT):
                    ins = dve.bn_stats(stats[:, n, :], x[:, bass.ds(b * T + n * C, C)])
                ins.then_inc(stats_made, 1)
                dve.wait_ge(stats_made, r + 1)
                dve.sem_inc(passed, 1)
                for n in range(NT):
                    ins = dve.bn_aggr(mv[:, n, :], stats[:, n, :])
                ins.then_inc(mv_made, 1)

            def norm_apply(b, r):
                dve.wait_ge(rstd_made, r + 1)
                for n in range(NT):
                    ins = dve.tensor_scalar(xn[:, n * C:(n + 1) * C], x[:, bass.ds(b * T + n * C, C)],
                                            mv[:, n, 0:1], rstd[:, 1, n:n + 1], ALU.subtract, ALU.mult)
                ins.then_inc(xn_made, 1)

            def gate_scores(f):
                dve.wait_ge(eg_made, f + 1)
                dve.tensor_scalar(eg, eg, 1.0, None, ALU.add).then_inc(eg1_made, 1)
                dve.wait_ge(eg1_made, f + 1)
                dve.reciprocal(sg.rearrange("p n h -> p (n h)"), eg).then_inc(sg_made, 1)

            def keys_values(f):
                for h in range(H):
                    dve.wait_ge(a_hi_made, f * H + (h + 1))
                    dve.tensor_tensor(A_lo[:, h * T:(h + 1) * T], S[:, h % 2, :],
                                      A_hi[:, h * T:(h + 1) * T].bitcast(F32), ALU.subtract).then_inc(a_lo_made, 1)
                for n in range(NT):
                    dve.wait_ge(v_hi_made, f * NT + (n + 1))
                    dve.tensor_tensor(V[:, :, n, 1, :], TP[:, (n % 2) * 512:(n % 2) * 512 + 512].rearrange("p (h d) -> p h d", h=H),
                                      V[:, :, n, 0, :].bitcast(F32), ALU.subtract).then_inc(v_lo_made, 1)

            def run(layer, b, f, more):
                if more:
                    norm_stats(b + 1, f + (layer * NB + 1))
                keys_values(f)

                def step(st):
                    m = st.tile(1)
                    if m.live():
                        dve.wait_ge(s_made, f * NS + m.t + 1)
                        dve.tensor_reduce(mx[:, m.par:m.par + 1], S[:, m.par, :], AX.X, ALU.max, negate=True).then_inc(max_made, 1)
                    p = st.tile(0)
                    if p.live():
                        for i in range(2):
                            part = slice(i * 512, (i + 1) * 512)
                            dve.wait_ge(pT_hi_made, (f * NS + p.t) * 2 + (i + 1))
                            dve.tensor_tensor(pT_lo[:, p.par, part], TP[:, part], pT_hi[:, p.par, part].bitcast(F32),
                                              ALU.subtract).then_inc(pT_lo_made, 1)
                    a = st.tile(AHEAD)
                    if a.live():
                        dve.wait_ge(xs_hi_made, f * NS + a.t + 1)
                        dve.tensor_tensor(xs_lo[:, a.par, :], xT_ps, xs_hi[:, a.par, :].bitcast(F32),
                                          ALU.subtract).then_inc(xs_lo_made, 1)
                    o = st.tile(-1)
                    if o.live():
                        dve.wait_ge(p_made, f * NS + o.t + 1)
                        dve.reciprocal(rden[:, o.par:o.par + 1], den[:, bass.ds(o.t, 1)]).then_inc(rden_made, 1)
                        dve.wait_ge(rden_made, f * NS + o.t + 1)
                        dve.wait_ge(o_made, f * NS + o.t + 1)
                        if o.least >= 2:
                            dve.wait_ge(o_turned, f * NS + o.t - 1)
                        dve.tensor_scalar(o_sb[:, o.par, :], o_ps, rden[:, o.par:o.par + 1], None,
                                          ALU.mult).then_inc(o_normed, 1)
                    if more and st.s == LOGIT_STEP:
                        gate_scores(f + 1)

                def between(s):
                    if more and s == LN_STEP:
                        dve.wait_ge(scattered, (f + 1) * NDMA)
                        norm_apply(b + 1, f + (layer * NB + 1))

                pipeline(dve, step, between)

            def ffn(layer):
                norm_stats(0, 2 * layer * NB)
                norm_apply(0, 2 * layer * NB)
                gate_scores(layer * NB)
                runs(dve, layer, lambda b, f, more: run(layer, b, f, more))

            def time_mix(b):
                r = b + NB
                norm_stats(b, r)
                norm_apply(b, r)
                ch = Chain(dve, wkv_chain, b * WKV_CHAIN)
                now, last = xT[:, 1:1 + T], xT[:, 0:T]
                dve.wait_ge(xT_made, r + 1)
                ch.link(dve.tensor_tensor(area(0), now, last, ALU.subtract))
                for i in range(3):
                    dve.scalar_tensor_tensor(out=area(1 + i), in0=area(0), scalar=cols[:, 2 + i:3 + i], in1=last,
                                             op0=ALU.mult, op1=ALU.add).then_inc(mixed, 1)
                k, v = area(4), area(5)
                pp, aa, bb = area(0, T + 1), area(7, T + 1), area(4, T + 1)
                p_new, p_old = pp[:, 1:1 + T], pp[:, 0:T]
                tmp, e_r = xn[:, :], xT[:, 1:1 + T]
                w, u = cols[:, 5:6], cols[:, 1:2]
                dve.wait_ge(kvr_copied, b * 3 + 3)
                dve.wait_ge(mixed, b * 3 + 3)
                dve.memset(pp[:, 0:1], NEG_INF)
                dve.memset(aa[:, 0:1], 0.0)
                ch.link(dve.tensor_tensor_scan(p_new, w.broadcast_to([P, T]), k, NEG_INF, ALU.add, ALU.max))
                dve.scalar_tensor_tensor(out=area(1), in0=p_old, scalar=w, in1=p_new,
                                         op0=ALU.add, op1=ALU.subtract).then_inc(arg_made, 1)
                dve.tensor_tensor(area(2), k, p_new, ALU.subtract).then_inc(arg_made, 1)
                ch.link(dve.scalar_tensor_tensor(out=tmp, in0=k, scalar=u, in1=p_old, op0=ALU.add, op1=ALU.max))
                dve.tensor_tensor(area(3), p_old, tmp, ALU.subtract).then_inc(arg_made, 1)
                dve.scalar_tensor_tensor(out=area(6), in0=k, scalar=u, in1=tmp,
                                         op0=ALU.add, op1=ALU.subtract).then_inc(arg_made, 1)
                dve.wait_ge(exp_made, b * 4 + 2)
                dve.wait_ge(arg_made, b * 4 + 4)
                dve.memset(bb[:, 0:1], 0.0)
                ch.done(dve.tensor_tensor_scan(bb[:, 1:1 + T], area(1), area(2), 0.0, ALU.mult, ALU.add))
                ch.link(dve.tensor_tensor(tmp, area(2), v, ALU.mult))
                ch.link(dve.tensor_tensor_scan(aa[:, 1:1 + T], area(1), tmp, 0.0, ALU.mult, ALU.add))
                dve.wait_ge(exp_made, b * 4 + 4)
                ch.done(dve.tensor_tensor(area(1), area(3), aa[:, 0:T], ALU.mult))
                ch.done(dve.tensor_tensor(area(2), area(6), v, ALU.mult))
                ch.link(dve.tensor_tensor(tmp, area(3), bb[:, 0:T], ALU.mult))
                ch.done(dve.tensor_tensor(area(1), area(1), area(2), ALU.add))
                ch.link(dve.tensor_tensor(tmp, tmp, area(6), ALU.add))
                ch.link(dve.scalar_tensor_tensor(out=tmp, in0=e_r, scalar=1.0, in1=tmp, op0=ALU.add, op1=ALU.mult))
                ch.link(dve.reciprocal(tmp, tmp))
                assert ch.n == WKV_CHAIN, ch.n
                dve.tensor_tensor(area(2), area(1), tmp, ALU.mult).then_inc(rw_made, 1)
                dve.wait_ge(ro_made, b + 1)
                xb = x[:, bass.ds(b * T, T)]
                dve.tensor_tensor(xb, TP[:, :], xb, ALU.add).then_inc(wkv_done, 1)
                dve.wait_ge(wkv_done, b + 1)

            dve.wait_ge(cols_made, 2)
            dve.wait_ge(loaded, 16 * NLOAD)
            dve.wait_ge(zeroed, 48)
            dve.wait_ge(bias_made, 3)
            dve.wait_ge(g_copied, 1)
            ffn(0)
            dve.wait_ge(ffn_done, NB)
            with dve.Fori(0, NB) as b:
                time_mix(b)
            ffn(1)

        @block.tensor
        def _(pe):
            pe.wait_ge(loaded, 16 * NLOAD)
            pe.wait_ge(consts, NCONST)
            for i, w in enumerate((wq_raw, wk_raw)):
                for h in range(H):
                    pe.transpose(S[0:DH, i, h * C:(h + 1) * C], w[:, h * DH:(h + 1) * DH], ident[:, :])
            for i in range(4):
                ins = pe.transpose(TP[:, i * C:(i + 1) * C], rw_raw[:, i, :], ident[:, :])
            ins.then_inc(w_turned, 1)
            pe.wait_ge(w_copied, 3)
            for h in range(H):
                ins = pe.matmul(S[:, 0, h * C:(h + 1) * C], wkT[:, h, :], wqT[:, h, :], start=True, stop=True)
            ins.then_inc(g_made, 1)
            pe.wait_ge(g_copied, 1)
            pe.wait_ge(bias_made, 3)

            def turn(r):
                pe.wait_ge(xn_made, r + 1)
                for n in range(NT):
                    ins = pe.transpose(TP[:, n * P:(n + 1) * P], xn[:, n * C:(n + 1) * C], ident[:, :])
                ins.then_inc(xn_turned, 1)

            def xT_tile(n):
                return xT[:, 1 + n * P:1 + (n + 1) * P]

            def logits(f):
                for n in range(NT):
                    ins = pe.matmul(logit_ps[:, n * H:(n + 1) * H], xT_tile(n), ws[:, :], start=True, stop=True)
                ins.then_inc(logits_made, 1)

            def ranks(f):
                pe.wait_ge(mask_made, f + 1)
                m = mask_b[:, :, :].rearrange("p n h -> p (n h)")
                pe.matmul(rank_ps, tri[:, :], m, start=True, stop=False, skip_group_check=True)
                for d in range(1, NT):
                    pe.matmul(rank_ps[:, d * H:NT * H], ones[:, :], m[:, 0:(NT - d) * H], start=False,
                              stop=(d == NT - 1), skip_group_check=True)
                for n in range(NT):
                    ins = pe.matmul(count_ps, ones[:, :], mask_b[:, n, :], start=(n == 0), stop=(n == NT - 1))
                ins.then_inc(rank_made, 1)

            def keys_values(f):
                for h in range(H):
                    if h >= 2:
                        pe.wait_ge(a_lo_made, f * H + (h - 1))
                    for i in range(2):
                        ins = pe.matmul(S[:, h % 2, i * 512:(i + 1) * 512], GT[:, h, :],
                                        xT[:, 1 + i * 512:1 + (i + 1) * 512], start=True, stop=True)
                    ins.then_inc(a_made, 1)
                for n in range(NT):
                    if n >= 2:
                        pe.wait_ge(v_lo_made, f * NT + (n - 1))
                    pe.matmul(TP[:, (n % 2) * 512:(n % 2) * 512 + 512], xT_tile(n), wv[:, :],
                              start=True, stop=True).then_inc(v_made, 1)

            def head(b, t):
                return nc.values_load(head_of[0:1, bass.ds((b % 2) * 32 + t, 1)], engines=[pe.engine], min_val=0, max_val=H - 1,
                                      skip_runtime_bounds_check_because="it counts the heads that start no later than the "
                                      "tile, less one: head 0 always does, and there are H")

            def run(layer, b, f, more):
                r = f + (layer * NB + 1)
                keys_values(f)
                pe.wait_ge(slots_made, f + 1)
                pe.sem_inc(passed, 1)

                def step(st):
                    q, o, y = st.tile(1), st.tile(-1), st.tile(-BEHIND)
                    if q.live():
                        in_A = pe.snap(head(b, q.t) * T)
                    if o.live():
                        in_V = pe.snap(head(b, o.t) * (NT * 2 * DH))
                    if y.live():
                        in_wo = pe.snap(head(b, y.t) * C)
                    if q.live():
                        pe.wait_ge(xs_lo_made, f * NS + q.t + 1)
                        if q.least >= 2:
                            pe.wait_ge(p_made, f * NS + q.t - 1)
                        else:
                            pe.wait_ge(a_lo_made, (f + 1) * H)
                        for n, (xx, A) in enumerate(((xs_hi, A_hi), (xs_lo, A_hi), (xs_hi, A_lo))):
                            for i in range(2):
                                ins = pe.matmul(S[:, q.par, i * 512:(i + 1) * 512], xx[:, q.par, :],
                                                A[:, bass.ds(in_A + i * 512, 512)], start=(n == 0), stop=(n == 2))
                        ins.then_inc(s_made, 1)
                    a = st.tile(AHEAD)
                    if y.live():
                        pe.wait_ge(o_normed, f * NS + y.t + 1)
                        if y.least >= 1:
                            pe.wait_ge(y_copied, f * NS + y.t)
                        if a.least - 1 < NS:
                            pe.wait_ge(xs_lo_made, f * NS + a.t)
                        pe.transpose(oT_ps, o_sb[:, y.par, :], ident[:, :]).then_inc(o_turned, 1)
                    p = st.tile(0)
                    if p.live():
                        pe.wait_ge(p_made, f * NS + p.t + 1)
                        if more and st.s == TURN_STEP + 1:
                            pe.wait_ge(xT_made, r + 1)
                        for i in range(2):
                            if p.least >= 1:
                                pe.wait_ge(pT_lo_made, (f * NS + p.t) * 2 + (i - 1))
                            else:
                                pe.wait_ge(v_lo_made, (f + 1) * NT)
                            for n in range(4 * i, 4 * i + 4):
                                ins = pe.transpose(TP[:, n * P:(n + 1) * P], probs[:, p.par, n * P:(n + 1) * P], ident[:, :])
                            ins.then_inc(p_turned, 1)
                    if y.live():
                        pe.wait_ge(oT_copied, f * NS + y.t + 1)
                    if more and st.s == LOGIT_STEP:
                        logits(f + 1)
                    if more and st.s == RANK_STEP:
                        ranks(f + 1)
                    if y.live():
                        pe.matmul(y_ps, oT[:, y.par, :], wo[:, bass.ds(in_wo, C)], start=True, stop=False)
                        pe.matmul(y_ps, ones33[:, :], bias[:, bass.ds(in_wo, C)], start=False, stop=True).then_inc(y_made, 1)
                    if a.live():
                        pe.wait_ge(xs_loaded[a.par], (f * (16 - a.par) + a.same + 1) * 16)
                        if a.least >= 1 and not y.live():
                            pe.wait_ge(xs_lo_made, f * NS + a.t)
                        pe.transpose(xT_ps, xs[:, a.par, :], ident[:, :]).then_inc(xs_turned, 1)
                    if o.live():
                        pe.wait_ge(pT_lo_made, (f * NS + o.t) * 2 + 2)
                        if o.least >= 1:
                            pe.wait_ge(o_normed, f * NS + o.t)
                        Vf = V[:, :, :, :, :].rearrange("p h n a d -> p (h n a d)")
                        for i, pT in enumerate((pT_hi, pT_lo)):
                            for n in range(NT):
                                ins = pe.matmul(o_ps, pT[:, o.par, n * P:(n + 1) * P], Vf[:, bass.ds(in_V + n * 2 * DH, 2 * DH)],
                                                start=(i == 0 and n == 0), stop=(i == 1 and n == NT - 1))
                        ins.then_inc(o_made, 1)
                    if more and st.s == TURN_STEP:
                        pe.wait_ge(pT_lo_made, (f * NS + (TURN_STEP + 1)) * 2)
                        turn(r)

                pipeline(pe, step, lambda s: None)
                pe.wait_ge(y_copied, (f + 1) * NS)

            def ffn(layer):
                f0, r0 = layer * NB, 2 * layer * NB
                turn(r0)
                pe.wait_ge(xT_made, r0 + 1)
                logits(f0)
                pe.wait_ge(eg_made, f0 + 1)
                ranks(f0)
                pe.wait_ge(rank_copied, f0 + 1)
                runs(pe, layer, lambda b, f, more: run(layer, b, f, more))

            ffn(0)
            with pe.Fori(0, NB) as b:
                turn(b + NB)
                for i, dst in enumerate((S[:, 0, :], S[:, 1, :], TP[:, :])):
                    pe.wait_ge(mixed, b * 3 + (i + 1))
                    for c in range(2):
                        ins = pe.matmul(dst[:, c * 512:(c + 1) * 512], rw_T[:, i, :], area(1 + i)[:, c * 512:(c + 1) * 512],
                                        start=True, stop=True)
                    ins.then_inc(kvr_made, 1)
                pe.wait_ge(rw_made, b + 1)
                for n in range(NT):
                    ins = pe.matmul(TP[:, n * C:(n + 1) * C], area(2)[:, n * P:(n + 1) * P], rw_T[:, 3, :],
                                    start=True, stop=True)
                ins.then_inc(ro_made, 1)
                pe.wait_ge(wkv_done, b + 1)
            ffn(1)


_INS = ['L0_attn_x', 'L0_attn_time_decay', 'L0_attn_time_first', 'L0_attn_time_mix_k', 'L0_attn_time_mix_v',
        'L0_attn_time_mix_r', 'L0_attn_Wk', 'L0_attn_Wv', 'L0_attn_Wr', 'L0_attn_Wo', 'L0_ffn_Wq', 'L0_ffn_Wkv',
        'L0_ffn_Ws', 'L0_ffn_Wo', 'L0_ffn_bo']
_OUTS = [((8, 1024, 128), 'float32')]


def kernel(**inputs):
    import numpy as _np
    import concourse.bacc as _bacc
    from concourse import mybir as _mybir
    from concourse.bass_utils import run_bass_kernel_spmd as _run

    nc = _bacc.Bacc("TRN2", target_bir_lowering=False, num_devices=1)
    arrays, args = {}, []
    for name in _INS:
        a = _np.ascontiguousarray(inputs[name])
        arrays[f"in_{name}_dram"] = a
        args.append(nc.dram_tensor(f"in_{name}_dram", a.shape, _mybir.dt.from_np(a.dtype), kind="ExternalInput").ap())
    for i, (shape, dtype) in enumerate(_OUTS):
        dt = _mybir.dt.from_np(_np.dtype(dtype))
        args.append(nc.dram_tensor(f"out_{i}_dram", shape, dt, kind="ExternalOutput").ap())
    build(nc, *args)
    r = _run(nc, [arrays], core_ids=[0])
    got = tuple(r.results[0][f"out_{i}_dram"] for i in range(len(_OUTS)))
    return got[0]
```

```python
from contextlib import ExitStack

import concourse.bass as bass
from concourse import mybir

F32 = mybir.dt.float32
F32R = mybir.dt.float32r
BF16 = mybir.dt.bfloat16
I32 = mybir.dt.int32
U32 = mybir.dt.uint32
ALU = mybir.AluOpType
ACT = mybir.ActivationFunctionType
AX = mybir.AxisListType

P = 128
NB, T, C = 8, 1024, 128
NT = T // P
H, DH, TOPK = 8, 64, 3
NS = (TOPK * T + H * (P - 1)) // P
SLOTS = NS * P
EPS = 1e-5
NEG_INF = -1e38
SCALE = DH ** -0.5

GATE_CHAIN, WKV_CHAIN = 46, 5
WORK = 6336

AHEAD, SCORED, BEHIND = 3, 2, 2
TURN_STEP, LOGIT_STEP, RANK_STEP, BIAS_STEP, KEY_STEP = 8, 9, 15, 16, NS - SCORED
VALUE_TILES = {-3: (0, 1, 2), -2: (3, 4, 5), -1: (6, 7)}


class Chain:

    def __init__(self, eng, sem, start, passed=None):
        self.eng, self.sem, self.start, self.passed, self.n = eng, sem, start, passed, 0

    def done(self, ins):
        self.n += 1
        ins.then_inc(self.sem, 1)

    def wait(self):
        self.eng.wait_ge(self.sem, self.start + self.n)
        if self.passed is not None:
            self.eng.sem_inc(self.passed, 1)

    def link(self, ins):
        self.done(ins)
        self.wait()


class Tile:

    def __init__(self, t, least, half):
        self.t, self.least, self.par, self.same = t, least, least % 2, half

    def live(self):
        return 0 <= self.least < NS


class Step:

    def __init__(self, s, i=None):
        self.s, self.i = s, i

    def tile(self, c):
        t = self.s + c
        if self.i is None:
            return Tile(t, t, t // 2)
        return Tile(self.i * 2 + t, t, self.i + t // 2)


def pipeline(eng, step, between):
    s = -AHEAD
    for stop, looped in ((10, 0), (14, 1), (16, 0), (24, 1), (NS + BEHIND, 0)):
        if looped:
            with eng.Fori(0, (stop - s) // 2) as i:
                for par in range(2):
                    step(Step(s + par, i))
            s = stop
        while s < stop:
            between(s)
            step(Step(s))
            s += 1


def build(nc, x_in, time_decay, time_first, mix_k, mix_v, mix_r, rk_w, rv_w, rr_w, ro_w,
          q_w, kv_w, s_w, o_w, o_b, out):
    ctx = ExitStack()
    with ctx:
        def sb(name, shape, dt=F32):
            return ctx.enter_context(nc.sbuf_tensor(name, shape, dt))

        def sem(name):
            return ctx.enter_context(nc.semaphore(name))


        x_slots = nc.dram_tensor("x_slots", (2 * SLOTS, C), F32, kind="Internal").ap()
        y_slots = nc.dram_tensor("y_slots", (2 * SLOTS, C), F32, kind="Internal").ap()

        x = sb("x", [P, NB * T])
        with ExitStack() as early:
            def lent(name, n):
                return early.enter_context(nc.sbuf_tensor(name, [P, n], F32))

            k, v, e_r = lent("k", T), lent("v", T), lent("e_r", T)
            pp, aa, bb = lent("pp", T + 1), lent("aa", T + 1), lent("bb", T + 1)
            old_w, new_w, old_u, new_u = lent("old_w", T), lent("new_w", T), lent("old_u", T), lent("new_u", T)
            p_out, kv_w_new, kv_u_new, den_u, rw = (lent("p_out", T), lent("kv_w_new", T), lent("kv_u_new", T),
                                                  lent("den_u", T), lent("rw", T))
            w_now, w_last = lent("w_now", 3 * C), lent("w_last", 3 * C)
        A_hi = sb("A_hi", [P, H * T], F32R)
        A_lo = sb("A_lo", [P, H * T], F32R)
        V = sb("V", [P, H, NT, 2, DH], F32R)
        xn = sb("xn", [P, NT * C])
        xT = sb("xT", [P, 1 + T])
        pT = sb("pT", [P, 2, 2, T], F32R)
        V_now = sb("V_now", [P, 2, NT * 2 * DH], F32R)
        pT_hi, pT_lo = pT[:, :, 0, :], pT[:, :, 1, :]
        xs_hi = sb("xs_hi", [P, 2, P], F32R)
        xs_lo = sb("xs_lo", [P, 2, P], F32R)
        GT = sb("GT", [P, H, C])
        wv = sb("wv", [P, H * DH])
        wo = sb("wo", [P, H * C])
        bias = sb("bias", [NT * H, T])
        gT = sb("gT", [NT * H, P])
        ws = sb("ws", [P, H])
        ident = sb("ident", [P, P])
        tri = sb("tri", [P, P], BF16)
        ones = sb("ones", [P, P], BF16)
        lower = sb("lower", [P, H, H])
        steps = sb("steps", [P, H, H])
        tile_no = sb("tile_no", [1, 32])
        rw_T = sb("rw_T", [P, 4, C])
        cols = sb("cols", [P, 6])
        mx = sb("mx", [P, 2])
        den = sb("den", [P, NS + 1])
        rden = sb("rden", [P, 2])
        stats = sb("stats", [P, NT, 6])
        mv = sb("mv", [P, NT, 2])
        rstd = sb("rstd", [P, 2, NT])
        powr = sb("powr", [P, NT])
        mask_b = sb("mask_b", [P, NT, H], BF16)
        ranks_sb = sb("ranks_sb", [P, NT * H + H])
        nh = sb("nh", [P, 4, H])
        eg = sb("eg", [P, NT * H])[:, :]
        sg = sb("sg", [P, NT, H])[:, :, :]
        dense = sb("dense", [P, NT * H])
        flip = sb("flip", [P, 1])
        slot_f = sb("slot_f", [P, TOPK, NT])
        slot_next = sb("slot_next", [P, TOPK, NT], U32)
        slot_now = sb("slot_now", [P, TOPK, NT], U32)
        gate_next = sb("gate_next", [P, TOPK, NT])
        gate_now = sb("gate_now", [P, TOPK, NT])
        head_next = sb("head_next", [1, 32], I32)
        head_of = sb("head_of", [1, 2 * 32], I32)

        work = sb("work", [P, WORK])
        at = 0

        def take(*shape):
            nonlocal at
            n = 1
            for d in shape:
                n *= d
            names = "abc"[:len(shape)]
            v = work[:, at:at + n]
            at += n
            if len(shape) > 1:
                v = v.rearrange(f"p ({' '.join(names)}) -> p {' '.join(names)}", **dict(zip(names, shape)))
            return v

        probs = take(2, T)
        y_got = take(2, T)
        cmp1 = take(NT, H, H)
        cmp2 = take(NT, H, H)
        small = take(5, NT * H)
        oT = take(2, P)
        xs = take(2, C)
        y_sb = take(2, C)
        assert at <= work.shape[1], at
        at = 0
        wq_raw, wk_raw = take(512), take(512)
        wqT, wkT = take(H, C)[0:DH], take(H, C)[0:DH]
        zeros = take(C)
        rw_raw = take(4, C)
        ones_f, ones_h, iota_f = take(P), take(H, H), take(H * H + 32 + 160)
        iota_i = iota_f.bitcast(I32)
        assert at <= work.shape[1]

        S = ctx.enter_context(nc.psum_tensor("S", [P, 2, T], F32))
        TP = ctx.enter_context(nc.psum_tensor("TP", [P, T], F32))
        OB = ctx.enter_context(nc.psum_tensor("OB", [P, 512], F32))
        MB = ctx.enter_context(nc.psum_tensor("MB", [P, 512], F32))
        xT_ps, y_ps, gT_ps, b_ps = MB[:, 0:128], MB[:, 128:256], MB[0:NT * H, 256:384], MB[:, 256:384]
        logit_ps, rank_ps, count_ps = MB[:, 384:448], MB[:, 384:448], MB[:, 448:456]
        o_ps = OB[:, 0:2 * P]

        loaded, x_loaded, zeroed, consts, pool_setup = sem("loaded"), sem("x_loaded"), sem("zeroed"), sem("consts"), sem("pool_setup")
        w_turned, w_copied = sem("w_turned"), sem("w_copied")
        g_made, g_copied = sem("g_made"), sem("g_copied")
        cols_made, bias_made = sem("cols_made"), sem("bias_made")
        stats_made, mv_made, rstd_made, xn_made = sem("stats_made"), sem("mv_made"), sem("rstd_made"), sem("xn_made")
        half_turned, half_xT_made = sem("half_turned"), sem("half_xT_made")
        centred, xn_turned, xT_made = sem("centred"), sem("xn_turned"), sem("xT_made")
        logits_made, eg_made, eg1_made, sg_made = sem("logits_made"), sem("eg_made"), sem("eg1_made"), sem("sg_made")
        mask_made, rank_made, rank_copied = sem("mask_made"), sem("rank_made"), sem("rank_copied")
        slots_made, scattered = sem("slots_made"), sem("scattered")
        a_made, a_hi_made, a_lo_made = sem("a_made"), sem("a_hi_made"), sem("a_lo_made")
        v_made, v_hi_made, v_lo_made = sem("v_made"), sem("v_hi_made"), sem("v_lo_made")
        xs_loaded = [sem(f"xs_loaded{i}") for i in range(2)]
        xs_turned, xs_hi_made, xs_lo_made = sem("xs_turned"), sem("xs_hi_made"), sem("xs_lo_made")
        s_made, max_made, p_made = sem("s_made"), sem("max_made"), sem("p_made")
        p_turned, pT_hi_made, pT_lo_made = sem("p_turned"), sem("pT_hi_made"), sem("pT_lo_made")
        v_now_made, o_made, rden_made, oT_made = sem("v_now_made"), sem("o_made"), sem("rden_made"), sem("oT_made")
        oT_half, y_made, y_copied = sem("oT_half"), sem("y_made"), sem("y_copied")
        dense_made, gT_turned, gT_made, b_made, b_added = (sem("dense_made"), sem("gT_turned"), sem("gT_made"),
                                                           sem("b_made"), sem("b_added"))
        y_stored = [sem(f"y_stored{i}") for i in range(2)]
        y_gathered, ffn_done = [sem(f"y_gathered{j}") for j in range(TOPK)], sem("ffn_done")
        mix_made, kvr_made, kvr_copied = sem("mix_made"), sem("kvr_made"), sem("kvr_copied")
        p_scanned, p_out_made = sem("p_scanned"), sem("p_out_made")
        arg_made, arg_made_p, exp_made = sem("arg_made"), sem("arg_made_p"), sem("exp_made")
        a_scanned, old_made = sem("a_scanned"), sem("old_made")
        kv_made, div_made, rw_made, ro_made, wkv_done = (sem("kv_made"), sem("div_made"), sem("rw_made"),
                                                         sem("ro_made"), sem("wkv_done"))
        gate_chain, wkv_chain, add_chain, pow_chain = (sem("gate_chain"), sem("wkv_chain"), sem("add_chain"),
                                                       sem("pow_chain"))
        stored, y_used, last_chain, last_done, last_stored = sem("stored"), sem("y_used"), sem("last_chain"), sem("last_done"), sem("last_stored")
        passed = sem("passed")

        NCONST = 13
        NLOAD = 1 + 6 + 4 + 5
        NDMA = TOPK * NT * 16
        COMBINE = 8

        block = ctx.enter_context(nc.Block())

        V_all = V[:, :, :, :, :].rearrange("p h n a d -> p (h n a d)")

        def head_on(eng, b, t):
            return nc.values_load(head_of[0:1, bass.ds((b % 2) * 32 + t, 1)], engines=[eng.engine], min_val=0, max_val=H - 1,
                                  skip_runtime_bounds_check_because="it counts the heads that start no later than the "
                                  "tile, less one: head 0 always does, and there are H")

        def key_heads(s):
            return range(2 * (s - KEY_STEP), 2 * (s - KEY_STEP) + 2)

        def runs(eng, layer, run):
            with eng.Fori(0, NB - 1) as b:
                run(b, b + layer * NB, True)
            run(NB - 1, NB - 1 + layer * NB, False)

        @block.sync
        def _(sp):
            def load_x(b, sem):
                sp.dma_start(x[:, b * T:(b + 1) * T].rearrange("p (n c) -> p n c", c=C),
                             x_in[b].rearrange("(n p) c -> p n c", p=P)).then_inc(sem, 16)

            load_x(0, loaded)
            sp.dma_start(wq_raw, q_w).then_inc(loaded, 16)
            sp.dma_start(wk_raw, kv_w[:, 0:512]).then_inc(loaded, 16)
            sp.dma_start(wv[:, :], kv_w[:, 512:1024]).then_inc(loaded, 16)
            sp.dma_start(ws[:, :], s_w).then_inc(loaded, 16)
            for i in range(2):
                sp.dma_start(wo[i * DH:(i + 1) * DH, :].rearrange("d (h e) -> d h e", h=H),
                             o_w.rearrange("h d e -> d h e")).then_inc(loaded, 16)
            sp.wait_ge(bias_made, 1)
            for n in range(NT):
                sp.dma_start(bias[n * H:(n + 1) * H, n * C:(n + 1) * C], o_b).then_inc(bias_made, 16)
            for i, w in enumerate((rk_w, rv_w, rr_w, ro_w)):
                sp.dma_start(rw_raw[:, i, :], w).then_inc(loaded, 16)
            for i, v in enumerate((time_decay, time_first)):
                sp.dma_start(cols[:, i:i + 1], v.rearrange("(c o) -> c o", o=1)).then_inc(loaded, 16)
            for i, v in enumerate((mix_k, mix_v, mix_r)):
                sp.dma_start(cols[:, 2 + i:3 + i], v.rearrange("a b c -> c (a b)")).then_inc(loaded, 16)
            sp.wait_ge(pool_setup, 1)
            for half in (x_slots[0:SLOTS], x_slots[SLOTS:2 * SLOTS], y_slots[SLOTS:2 * SLOTS]):
                sp.dma_start(half.rearrange("(n p) c -> p n c", p=P),
                             zeros.unsqueeze(1).broadcast_to([P, NS, C])).then_inc(zeroed, 16)

            for b in range(1, NB):
                load_x(b, x_loaded)

            def load(b, f, a):
                first = (b % 2) * SLOTS
                sp.dma_start(xs[:, a.par, :], x_slots[bass.ds(first + a.t * P, P), :]).then_inc(xs_loaded[a.par], 16)

            def load_first_two(b, f):
                sp.wait_ge(scattered, (f + 1) * NDMA)
                for t in range(2):
                    load(b, f, Tile(t, t, 0))

            def run(b, f, more):
                def step(st):
                    a = st.tile(AHEAD + 1)
                    if a.least >= 2 and a.live():
                        sp.wait_ge(xs_turned, f * NS + a.t - 1)
                        load(b, f, a)
                    if more and st.s == NS:
                        sp.wait_ge(xs_turned, f * NS + NS)
                        load_first_two(b + 1, f + 1)
                    y = st.tile(-BEHIND)
                    if y.live():
                        sp.wait_ge(y_copied, f * NS + y.t + 1)
                        sp.dma_start(y_slots[bass.ds((b % 2) * SLOTS + y.t * P, P), :], y_sb[:, y.par, :]).then_inc(y_stored[y.par], 16)

                pipeline(sp, step, lambda s: None)

            for layer in range(2):
                load_first_two(0, layer * NB)
                runs(sp, layer, run)
            sp.wait_ge(last_done, 1)
            b = NB - 1
            sp.dma_start(out[b].rearrange("(n p) c -> p n c", p=P),
                         x[:, b * T:(b + 1) * T].rearrange("p (n c) -> p n c", c=C)).then_inc(last_stored, 16)
            sp.wait_ge(stored, 16 * (NB - 1))
            sp.wait_ge(last_stored, 16)

        @block.gpsimd
        def _(pool):
            pool.memset(zeros, 0.0).then_inc(pool_setup, 1)
            pool.memset(ones_f, 1.0).then_inc(consts, 1)
            pool.memset(ones[:, :], 1.0).then_inc(consts, 1)
            pool.memset(powr[:, :], -0.5).then_inc(consts, 1)
            pool.memset(xT[:, 0:1], 0.0).then_inc(consts, 1)
            pool.memset(ones_h, 1.0).then_inc(consts, 1)
            pool.memset(flip[:, :], float(SLOTS)).then_inc(consts, 1)
            pool.wait_ge(consts, 6)
            pool.affine_select(out=ident[:, :], in_=ones_f, compare_op=ALU.is_equal, fill=0.0, base=0,
                               pattern=[[-1, P]], channel_multiplier=1).then_inc(consts, 1)
            pool.affine_select(out=tri[:, :], in_=ones[:, :], compare_op=ALU.is_gt, fill=0.0, base=0,
                               pattern=[[1, P]], channel_multiplier=-1).then_inc(consts, 1)
            pool.affine_select(out=lower[:, :, :], in_=ones_h, compare_op=ALU.is_gt, fill=0.0, base=0,
                               pattern=[[1, H], [-1, H]], channel_multiplier=0).then_inc(consts, 1)
            pool.iota(iota_i[:, 0:H * H], [[0, H], [P, H]], base=0, channel_multiplier=0).then_inc(consts, 1)
            pool.iota(iota_i[:, H * H:H * H + 32], [[1, 32]], base=0, channel_multiplier=0).then_inc(consts, 1)
            pool.wait_ge(consts, 11)
            pool.tensor_copy(steps[:, :, :].rearrange("p a b -> p (a b)"), iota_i[:, 0:H * H]).then_inc(consts, 1)
            pool.tensor_copy(tile_no[:, :], iota_i[0:1, H * H:H * H + 32]).then_inc(consts, 1)

            def root(r):
                pool.wait_ge(mv_made, r + 1)
                pool.sem_inc(passed, 1)
                pool.tensor_scalar(rstd[:, 0, :], mv[:, :, 1], EPS, None, ALU.add).then_inc(pow_chain, 1)
                pool.wait_ge(pow_chain, r + 1)
                pool.tensor_tensor(rstd[:, 1, :], rstd[:, 0, :], powr[:, :], ALU.pow).then_inc(rstd_made, 1)

            def gates(b, f, first=False):
                ch = Chain(pool, gate_chain, f * GATE_CHAIN, passed)
                low = lower[:, :, :].unsqueeze(1).broadcast_to([P, NT, H, H])

                def total(src, tmp, dst):
                    ch.link(pool.tensor_tensor(tmp[..., 0:4], src[..., 0:4], src[..., 4:8], ALU.add))
                    ch.link(pool.tensor_tensor(tmp[..., 0:2], tmp[..., 0:2], tmp[..., 2:4], ALU.add))
                    ch.link(pool.tensor_tensor(dst, tmp[..., 0:1], tmp[..., 1:2], ALU.add))

                def by_head(i):
                    return small[:, i, :].rearrange("p (n h) -> p n h", h=H)

                c1 = cmp1
                c2 = cmp2
                before, mask, chosen_before, slot, not_chosen = (by_head(i) for i in range(5))
                half = before
                sel, pick, tmp = (c.rearrange("p a b c -> p (a b c)")[:, at:at + TOPK * NT * H]
                                  .rearrange("p (j n h) -> p j n h", j=TOPK, n=NT) for c, at in ((cmp1, 0), (cmp1, 256), (cmp2, 0)))
                dense_w = dense[:, :].rearrange("p (n h) -> p n h", h=H)
                pool.wait_ge(sg_made, f + 1)
                pool.sem_inc(passed, 1)
                g_of = sg.unsqueeze(2).broadcast_to([P, NT, H, H])
                h_of = sg.unsqueeze(3).broadcast_to([P, NT, H, H])
                ch.link(pool.tensor_tensor(c1, g_of, h_of, ALU.subtract))
                ch.link(pool.tensor_scalar(c2, c1, 0.0, None, ALU.is_equal))
                ch.link(pool.tensor_tensor(c2, c2, low, ALU.mult))
                ch.link(pool.tensor_scalar(c1, c1, 0.0, None, ALU.is_gt))
                ch.link(pool.tensor_tensor(c1, c1, c2, ALU.add))
                total(c1, c2, before.unsqueeze(3))
                ch.link(pool.tensor_scalar(mask, before, float(TOPK), None, ALU.is_lt))
                ch.link(pool.tensor_scalar(half, sg, 0.5, None, ALU.mult))
                pool.tensor_tensor(dense_w, mask, half, ALU.mult).then_inc(dense_made, 1)
                pool.tensor_copy(mask_b[:, :, :], mask).then_inc(mask_made, 1)
                ch.link(pool.tensor_tensor(c1, mask.unsqueeze(2).broadcast_to([P, NT, H, H]), low, ALU.mult))
                total(c1, c2, chosen_before.unsqueeze(3))
                ch.link(pool.tensor_scalar(not_chosen, mask, -float(H), float(H), ALU.mult, ALU.add))
                ch.link(pool.tensor_tensor(chosen_before, chosen_before, not_chosen, ALU.add))
                pool.wait_ge(rank_copied, f + 1)
                pool.sem_inc(passed, 1)
                count = ranks_sb[:, NT * H:].unsqueeze(2).broadcast_to([P, H, H])
                m1, m2 = c1[:, 0], c2[:, 0]
                tiles, first_tile = nh[:, 0], nh[:, 1]
                ch.link(pool.tensor_tensor(m1, count, steps[:, :, :], ALU.subtract))
                ch.link(pool.tensor_scalar(m1, m1, 0.0, None, ALU.is_gt))
                total(m1, m2, tiles.unsqueeze(2))
                ch.link(pool.tensor_tensor(m1, tiles.unsqueeze(1).broadcast_to([P, H, H]), lower[:, :, :], ALU.mult))
                total(m1, m2, first_tile.unsqueeze(2))
                t1 = c1[0:1, 0:4].rearrange("p a b c -> p (a b) c")
                t2 = c2[0:1, 0:4].rearrange("p a b c -> p (a b) c")
                t3 = c2[0:1, 4, 0:4].rearrange("p a b -> p (a b)").unsqueeze(2)
                ch.link(pool.tensor_tensor(t1, tile_no[:, :].unsqueeze(2).broadcast_to([1, 32, H]),
                                           first_tile[0:1].unsqueeze(1).broadcast_to([1, 32, H]), ALU.subtract))
                ch.link(pool.tensor_scalar(t1, t1, 0.0, None, ALU.is_ge))
                total(t1, t2, t3)
                ch.link(pool.tensor_scalar(head_next[:, :].unsqueeze(2), t3, -1.0, None, ALU.add))
                ch.done(pool.tensor_copy(head_of[:, bass.ds((b % 2) * 32, 32)], head_next[:, :]))
                ch.link(pool.tensor_scalar(flip[:, :], flip[:, :], -1.0, float(SLOTS), ALU.mult, ALU.add))
                ch.link(pool.tensor_scalar(first_tile, first_tile, float(P), None, ALU.mult))
                ch.link(pool.tensor_tensor(slot, first_tile.unsqueeze(1).broadcast_to([P, NT, H]),
                                           ranks_sb[:, 0:NT * H].rearrange("p (n h) -> p n h", h=H), ALU.add))
                for j in range(TOPK):
                    ins = pool.tensor_scalar(sel[:, j], chosen_before, float(j), None, ALU.is_equal)
                    if j < TOPK - 1:
                        ch.done(ins)
                    else:
                        ch.link(ins)
                each = [P, TOPK, NT, H]
                ch.link(pool.tensor_tensor(pick, sel, slot.unsqueeze(1).broadcast_to(each), ALU.mult))
                total(pick, tmp, slot_f[:, :, :].unsqueeze(3))
                pool.tensor_scalar(slot_next[:, :, :], slot_f[:, :, :], flip[:, 0:1], None, ALU.add).then_inc(slots_made, 1)
                pool.wait_ge(slots_made, f + 1)
                pool.sem_inc(passed, 1)
                if first:
                    pool.wait_ge(zeroed, 48)
                    pool.sem_inc(passed, 1)
                for j in range(TOPK):
                    for n in range(NT):
                        pool.indirect_dma_start(
                            out=x_slots, out_offset=bass.IndirectOffsetOnAxis(ap=slot_next[:, j, n:n + 1], axis=0),
                            in_=xn[:, n * C:(n + 1) * C], in_offset=None).then_inc(scattered, 16)
                ch.link(pool.tensor_tensor(pick, sel, half.unsqueeze(1).broadcast_to(each), ALU.mult))
                total(pick, tmp, gate_next[:, :, :].unsqueeze(3))
                assert ch.n == GATE_CHAIN, ch.n

            def turn_over(f):
                ch = Chain(pool, add_chain, f * COMBINE)
                ch.done(pool.tensor_copy(slot_now[:, :, :], slot_next[:, :, :]))
                ch.link(pool.tensor_copy(gate_now[:, :, :], gate_next[:, :, :]))

            def gather(f, j):
                for n in range(NT):
                    pool.indirect_dma_start(
                        out=y_got[:, j % 2, n * C:(n + 1) * C], out_offset=None, in_=y_slots,
                        in_offset=bass.IndirectOffsetOnAxis(ap=slot_now[:, j, n:n + 1], axis=0)).then_inc(y_gathered[j], 16)

            def gather_two(f):
                pool.wait_ge(y_stored[0], (f + 1) * (16 * 16))
                pool.wait_ge(y_stored[1], (f + 1) * (15 * 16))
                pool.sem_inc(passed, 1)
                gather(f, 0)
                gather(f, 1)

            def combine(b, f):
                xb = x[:, bass.ds(b * T, T)]
                ch = Chain(pool, add_chain, f * COMBINE + 2, passed)
                pool.wait_ge(b_added, (f + 1) * NT)
                for j in range(TOPK):
                    y = y_got[:, j % 2, :].rearrange("p (n c) -> p n c", c=C)
                    pool.wait_ge(y_gathered[j], (f + 1) * (NT * 16))
                    g = gate_now[:, j, :].unsqueeze(2).broadcast_to([P, NT, C])
                    ch.link(pool.tensor_tensor(y, y, g, ALU.mult))
                    ch.link(pool.tensor_tensor(xb, xb, y_got[:, j % 2, :], ALU.add))
                    if j + 2 < TOPK:
                        pool.sem_inc(passed, 1)
                        gather(f, j + 2)
                assert ch.n == COMBINE - 2
                pool.sem_inc(ffn_done, 1)

            def ffn(layer):
                f0 = layer * NB
                if layer == 0:
                    root(0)
                gates(0, f0, layer == 0)
                turn_over(f0)

                def run(b, f, more):
                    if more:
                        root(f + (layer * NB + 1))
                        pool.wait_ge(scattered, (f + 1) * NDMA)
                        pool.sem_inc(passed, 1)
                        normed = xn[:, :].rearrange("p (n c) -> p n c", c=C)
                        pool.tensor_tensor(normed, x[:, bass.ds((b + 1) * T, T)].rearrange("p (n c) -> p n c", c=C),
                                           mv[:, :, 0:1].broadcast_to([P, NT, C]), ALU.subtract).then_inc(centred, 1)
                        pool.wait_ge(centred, f + (1 - layer))
                        pool.wait_ge(rstd_made, f + (layer * NB + 2))
                        pool.sem_inc(passed, 1)
                        pool.tensor_tensor(normed, normed, rstd[:, 1, :].unsqueeze(2).broadcast_to([P, NT, C]),
                                           ALU.mult).then_inc(xn_made, 1)
                        gates(b + 1, f + 1)
                    elif layer == 0:
                        return
                    gather_two(f)
                    if not more:
                        pool.wait_ge(y_used, 1)
                        gather(f, 2)
                        return
                    combine(b, f)
                    if layer == 1:
                        xb = x[:, bass.ds(b * T, T)]
                        pool.dma_start(out[bass.ds(b, 1)].rearrange("o (n p) c -> p (o n) c", p=P),
                                       xb.rearrange("p (n c) -> p n c", c=C)).then_inc(stored, 16)
                    if more:
                        turn_over(f + 1)

                runs(pool, layer, run)

            pool.wait_ge(g_copied, 1)
            ffn(0)
            def time_mix(b):
                root(b + (NB + 1))
                pool.wait_ge(p_scanned, b + 1)
                pool.tensor_tensor(new_w[:, :], k[:, :], pp[:, 1:1 + T], ALU.subtract).then_inc(arg_made_p, 1)
                pool.wait_ge(p_out_made, b + 1)
                pool.tensor_tensor(old_u[:, :], pp[:, 0:T], p_out[:, :], ALU.subtract).then_inc(arg_made_p, 1)
                pool.wait_ge(exp_made, b * 4 + 2)
                pool.tensor_tensor(kv_w_new[:, :], new_w[:, :], v[:, :], ALU.mult).then_inc(kv_made, 1)
                pool.wait_ge(exp_made, b * 4 + 4)
                pool.tensor_tensor(kv_u_new[:, :], new_u[:, :], v[:, :], ALU.mult).then_inc(kv_made, 1)
                pool.wait_ge(a_scanned, b + 1)
                pool.tensor_tensor(aa[:, 0:T], old_u[:, :], aa[:, 0:T], ALU.mult).then_inc(old_made, 1)

            root(NB)
            gather_two(NB - 1)
            time_mix(0)
            combine(NB - 1, NB - 1)
            with pool.Fori(1, NB - 1) as b:
                time_mix(b)
            time_mix(NB - 1)
            ffn(1)

        @block.scalar
        def _(act):
            act.wait_ge(w_turned, 1)
            act.activation(wqT.rearrange("p h c -> p (h c)"), S[0:DH, 0, :], ACT.Copy).then_inc(w_copied, 1)
            act.activation(wkT.rearrange("p h c -> p (h c)"), S[0:DH, 1, :], ACT.Copy).then_inc(w_copied, 1)
            act.activation(rw_T[:, :, :].rearrange("p a b -> p (a b)"), TP[:, 0:512], ACT.Copy).then_inc(w_copied, 1)
            act.wait_ge(g_made, 1)
            act.activation(GT[:, :, :].rearrange("p h c -> p (h c)"), S[:, 0, :], ACT.Copy, scale=SCALE).then_inc(g_copied, 1)
            act.wait_ge(loaded, 16 * NLOAD)
            act.activation(cols[:, 5:6], cols[:, 0:1], ACT.Exp).then_inc(cols_made, 1)

            def transpose_out(r):
                act.wait_ge(xn_turned, r + 1)
                act.activation(xT[:, 1:1 + T], TP[:, :], ACT.Copy).then_inc(xT_made, 1)

            def gate_exp(f):
                act.wait_ge(logits_made, f + 1)
                act.activation(eg, logit_ps, ACT.Exp, scale=-1.0).then_inc(eg_made, 1)

            def rank_copy(f):
                act.wait_ge(rank_made, f + 1)
                act.activation(ranks_sb[:, :], MB[:, 384:456], ACT.Copy).then_inc(rank_copied, 1)

            def keys(f, heads):
                for h in heads:
                    act.wait_ge(a_made, f * H + (h + 1))
                    act.activation(A_hi[:, h * T:(h + 1) * T], S[:, h % 2, :], ACT.Copy).then_inc(a_hi_made, 1)

            def values(f, tiles):
                for n in tiles:
                    act.wait_ge(v_made, f * NT + (n + 1))
                    act.activation(V[:, :, n, 0, :], TP[:, (n % 2) * 512:(n % 2) * 512 + 512].rearrange("p (h d) -> p h d", h=H),
                                   ACT.Copy).then_inc(v_hi_made, 1)

            def weights_turned_out(f):
                act.wait_ge(gT_turned, f + 1)
                act.activation(gT[:, :], gT_ps, ACT.Copy).then_inc(gT_made, 1)

            def run(layer, b, f, more):
                act.wait_ge(slots_made, f + 1)
                act.sem_inc(passed, 1)

                def step(st):
                    a, e, p, y = (st.tile(c) for c in (AHEAD, 1, 0, -BEHIND))
                    if more and st.s > KEY_STEP:
                        keys(f + 1, key_heads(st.s - 1))
                    if p.live():
                        for i in range(2):
                            act.wait_ge(p_turned, (f * NS + p.t) * 2 + (i + 1))
                            if p.least >= 2:
                                act.wait_ge(o_made, f * NS + p.t - 1)
                            act.activation(pT_hi[:, p.par, i * 512:(i + 1) * 512], TP[:, i * 512:(i + 1) * 512],
                                           ACT.Copy).then_inc(pT_hi_made, 1)
                    if e.live():
                        act.wait_ge(max_made, f * NS + e.t + 1)
                        if e.least >= 2:
                            act.wait_ge(p_turned, (f * NS + e.t) * 2 - 2)
                        act.activation(probs[:, e.par, :], S[:, e.par, :], ACT.Exp, bias=mx[:, e.par:e.par + 1],
                                       accum_out=den[:, bass.ds(e.t, 1)]).then_inc(p_made, 1)
                    if y.live():
                        act.wait_ge(y_made, f * NS + y.t + 1)
                        act.wait_ge(rden_made, f * NS + y.t + 1)
                        if a.live():
                            act.wait_ge(xs_turned, f * NS + a.t + 1)
                        if more and st.s == LOGIT_STEP:
                            gate_exp(f + 1)
                        if more and st.s == RANK_STEP:
                            rank_copy(f + 1)
                            weights_turned_out(f + 1)
                        if y.least >= 2:
                            act.wait_ge(y_stored[y.par], (f * (16 - y.par) + y.same) * 16)
                        act.activation(y_sb[:, y.par, :], y_ps, ACT.Copy, scale=rden[:, y.par:y.par + 1]).then_inc(y_copied, 1)
                    if a.live():
                        act.wait_ge(xs_turned, f * NS + a.t + 1)
                        if a.least >= 2:
                            act.wait_ge(s_made, f * NS + a.t - 1)
                        act.activation(xs_hi[:, a.par, :], xT_ps, ACT.Copy).then_inc(xs_hi_made, 1)
                    if p.live():
                        in_V = act.snap(head_on(act, b, p.t) * (NT * 2 * DH))
                        act.activation(V_now[:, p.par, :], V_all[:, bass.ds(in_V, NT * 2 * DH)].bitcast(F32),
                                       ACT.Copy).then_inc(v_now_made, 1)
                    if more and st.s == TURN_STEP:
                        act.wait_ge(half_turned, f + (1 - layer))
                        act.activation(xT[:, 1:1 + 512], TP[:, 0:512], ACT.Copy).then_inc(half_xT_made, 1)
                        act.wait_ge(xn_turned, f + (layer * NB + 2))
                        act.activation(xT[:, 513:1 + T], TP[:, 512:T], ACT.Copy).then_inc(xT_made, 1)
                    if st.s in VALUE_TILES:
                        values(f, VALUE_TILES[st.s])

                pipeline(act, step, lambda s: None)
                if more:
                    keys(f + 1, key_heads(NS + BEHIND - 1))

            def ffn(layer):
                f0 = layer * NB
                if layer == 0:
                    transpose_out(0)
                    gate_exp(0)
                rank_copy(f0)
                weights_turned_out(f0)
                keys(f0, range(H))
                runs(act, layer, lambda b, f, more: run(layer, b, f, more))

            ffn(0)

            def front(b):
                act.wait_ge(xn_turned, b + (NB + 1))
                act.activation(xT[:, 1:1 + 512], OB[:, :], ACT.Copy)
                act.activation(xT[:, 513:1 + T], MB[:, :], ACT.Copy).then_inc(xT_made, 1)

            def copy_kvr(b, first):
                act.wait_ge(kvr_made, b * 3 + 1)
                act.activation(k[:, :], S[:, 0, :], ACT.Copy).then_inc(kvr_copied, 1)
                act.wait_ge(kvr_made, b * 3 + 2)
                if not first:
                    act.wait_ge(kv_made, b * 2)
                act.activation(v[:, :], S[:, 1, :], ACT.Copy).then_inc(kvr_copied, 1)
                act.wait_ge(kvr_made, b * 3 + 3)
                if not first:
                    act.wait_ge(div_made, b)
                act.activation(e_r[:, :], TP[:, :], ACT.Exp, scale=-1.0).then_inc(kvr_copied, 1)

            def time_mix(b, more):
                for to, made, n in ((old_w, arg_made, 1), (new_w, arg_made_p, 1), (new_u, arg_made, 2), (old_u, arg_made_p, 2)):
                    act.wait_ge(made, b * 2 + n)
                    act.activation(to[:, :], to[:, :], ACT.Exp).then_inc(exp_made, 1)
                front(b + 1)
                if more:
                    copy_kvr(b + 1, False)
                else:
                    gate_exp(NB)

            front(0)
            copy_kvr(0, True)
            with act.Fori(0, NB - 1) as b:
                time_mix(b, True)
            time_mix(NB - 1, False)
            ffn(1)

        @block.vector
        def _(dve):
            dve.memset(bias[:, :], 0.0).then_inc(bias_made, 1)
            dve.wait_ge(cols_made, 1)
            dve.wait_ge(consts, NCONST)
            dve.tensor_scalar(cols[:, 5:6], cols[:, 5:6], -1.0, None, ALU.mult).then_inc(cols_made, 1)
            dve.wait_ge(cols_made, 2)

            def norm_stats(b, r):
                for n in range(NT):
                    ins = dve.bn_stats(stats[:, n, :], x[:, bass.ds(b * T + n * C, C)])
                ins.then_inc(stats_made, 1)
                dve.wait_ge(stats_made, r + 1)
                dve.sem_inc(passed, 1)
                for n in range(NT):
                    ins = dve.bn_aggr(mv[:, n, :], stats[:, n, :])
                ins.then_inc(mv_made, 1)

            def norm_stats_step(b, r, s):
                n = s + AHEAD
                if n < NT:
                    ins = dve.bn_stats(stats[:, n, :], x[:, bass.ds(b * T + n * C, C)])
                    if n == NT - 1:
                        ins.then_inc(stats_made, 1)
                elif n == NT:
                    dve.wait_ge(stats_made, r + 1)
                    dve.sem_inc(passed, 1)
                    for m in range(NT):
                        ins = dve.bn_aggr(mv[:, m, :], stats[:, m, :])
                    ins.then_inc(mv_made, 1)

            def norm_apply(b, r):
                dve.wait_ge(rstd_made, r + 1)
                for n in range(NT):
                    ins = dve.tensor_scalar(xn[:, n * C:(n + 1) * C], x[:, bass.ds(b * T + n * C, C)],
                                            mv[:, n, 0:1], rstd[:, 1, n:n + 1], ALU.subtract, ALU.mult)
                ins.then_inc(xn_made, 1)

            def gate_scores(f):
                dve.wait_ge(eg_made, f + 1)
                dve.tensor_scalar(eg, eg, 1.0, None, ALU.add).then_inc(eg1_made, 1)
                dve.wait_ge(eg1_made, f + 1)
                dve.reciprocal(sg.rearrange("p n h -> p (n h)"), eg).then_inc(sg_made, 1)

            def keys(f, heads):
                for h in heads:
                    dve.wait_ge(a_hi_made, f * H + (h + 1))
                    dve.tensor_tensor(A_lo[:, h * T:(h + 1) * T], S[:, h % 2, :],
                                      A_hi[:, h * T:(h + 1) * T].bitcast(F32), ALU.subtract).then_inc(a_lo_made, 1)

            def values(f, tiles):
                for n in tiles:
                    dve.wait_ge(v_hi_made, f * NT + (n + 1))
                    dve.tensor_tensor(V[:, :, n, 1, :], TP[:, (n % 2) * 512:(n % 2) * 512 + 512].rearrange("p (h d) -> p h d", h=H),
                                      V[:, :, n, 0, :].bitcast(F32), ALU.subtract).then_inc(v_lo_made, 1)

            def add_bias(b, layer):
                dve.wait_ge(b_made, layer + 1)
                xb = x[:, bass.ds(b * T, T)]
                dve.tensor_tensor(xb, TP[:, :], xb, ALU.add).then_inc(b_added, NT)

            def run(layer, b, f, more):
                def step(st):
                    o = st.tile(-BEHIND)
                    if o.live():
                        dve.wait_ge(p_made, f * NS + o.t + 1)
                        if o.least >= 2:
                            dve.wait_ge(y_copied, f * NS + o.t - 1)
                        dve.reciprocal(rden[:, o.par:o.par + 1], den[:, bass.ds(o.t, 1)]).then_inc(rden_made, 1)
                        dve.wait_ge(o_made, f * NS + o.t + 1)
                        dve.tensor_copy(oT[:, o.par, :], o_ps[:, 0:P]).then_inc(oT_half, 1)
                        dve.wait_ge(oT_half, f * NS + o.t + 1)
                        dve.tensor_tensor(oT[:, o.par, :], o_ps[:, P:2 * P], oT[:, o.par, :], ALU.add).then_inc(oT_made, 1)
                    if more and st.s > KEY_STEP:
                        keys(f + 1, key_heads(st.s - 1))
                    p = st.tile(0)
                    if p.live():
                        for i in range(2):
                            part = slice(i * 512, (i + 1) * 512)
                            dve.wait_ge(pT_hi_made, (f * NS + p.t) * 2 + (i + 1))
                            dve.tensor_tensor(pT_lo[:, p.par, part], TP[:, part], pT_hi[:, p.par, part].bitcast(F32),
                                              ALU.subtract).then_inc(pT_lo_made, 1)
                    m = st.tile(SCORED)
                    if m.live():
                        dve.wait_ge(s_made, f * NS + m.t + 1)
                        dve.tensor_reduce(mx[:, m.par:m.par + 1], S[:, m.par, :], AX.X, ALU.max, negate=True).then_inc(max_made, 1)
                    a = st.tile(AHEAD)
                    if a.live():
                        dve.wait_ge(xs_hi_made, f * NS + a.t + 1)
                        if more and BIAS_STEP <= st.s < BIAS_STEP + NT:
                            at = (b + 1) * T + (st.tile(-BIAS_STEP).t) * C
                            dve.tensor_tensor(x[:, bass.ds(at, C)], b_ps, x[:, bass.ds(at, C)], ALU.add).then_inc(b_added, 1)
                        dve.tensor_tensor(xs_lo[:, a.par, :], xT_ps, xs_hi[:, a.par, :].bitcast(F32),
                                          ALU.subtract).then_inc(xs_lo_made, 1)
                    if more and st.s == LOGIT_STEP:
                        gate_scores(f + 1)
                    if st.s in VALUE_TILES:
                        values(f, VALUE_TILES[st.s])

                def between(s):
                    if more:
                        norm_stats_step(b + 1, f + (layer * NB + 1), s)

                pipeline(dve, step, between)
                if more:
                    keys(f + 1, key_heads(NS + BEHIND - 1))

            def ffn(layer):
                if layer == 0:
                    norm_stats(0, 0)
                    norm_apply(0, 0)
                    gate_scores(0)
                add_bias(0, layer)
                keys(layer * NB, range(H))
                dve.wait_ge(x_loaded, 16 * (NB - 1))
                runs(dve, layer, lambda b, f, more: run(layer, b, f, more))

            def mix_weights():
                for i in range(3):
                    now, last = w_now[:, i * C:(i + 1) * C], w_last[:, i * C:(i + 1) * C]
                    dve.tensor_scalar(now, rw_T[:, i, :], cols[:, 2 + i:3 + i], None, ALU.mult).then_inc(mix_made, 1)
                    dve.wait_ge(mix_made, 2 * i + 1)
                    dve.tensor_tensor(last, rw_T[:, i, :], now, ALU.subtract).then_inc(mix_made, 1)
                dve.memset(pp[:, 0:1], NEG_INF).then_inc(mix_made, 1)
                dve.memset(aa[:, 0:1], 0.0).then_inc(mix_made, 1)
                dve.memset(bb[:, 0:1], 0.0).then_inc(mix_made, 1)
                dve.wait_ge(mix_made, 9)

            def add_out(b):
                dve.wait_ge(ro_made, b + 1)
                for i, bank in enumerate((OB, MB)):
                    xb = x[:, bass.ds(b * T + i * 512, 512)]
                    ins = dve.tensor_tensor(xb, bank[:, :], xb, ALU.add)
                ins.then_inc(wkv_done, 1)

            def time_mix(b, first, more):
                after = b + 1 if more else 0
                norm_stats(after, b + (NB + 1))
                ch = Chain(dve, wkv_chain, b * WKV_CHAIN)
                p_new, p_old = pp[:, 1:1 + T], pp[:, 0:T]
                w, u = cols[:, 5:6], cols[:, 1:2]
                dve.wait_ge(kvr_copied, b * 3 + 1)
                dve.tensor_tensor_scan(p_new, w.broadcast_to([P, T]), k[:, :], NEG_INF, ALU.add, ALU.max).then_inc(p_scanned, 1)
                dve.wait_ge(p_scanned, b + 1)
                dve.scalar_tensor_tensor(out=old_w[:, :], in0=p_old, scalar=w, in1=p_new,
                                         op0=ALU.add, op1=ALU.subtract).then_inc(arg_made, 1)
                dve.scalar_tensor_tensor(out=p_out[:, :], in0=k[:, :], scalar=u, in1=p_old,
                                         op0=ALU.add, op1=ALU.max).then_inc(p_out_made, 1)
                dve.wait_ge(p_out_made, b + 1)
                dve.scalar_tensor_tensor(out=new_u[:, :], in0=k[:, :], scalar=u, in1=p_out[:, :],
                                         op0=ALU.add, op1=ALU.subtract).then_inc(arg_made, 1)
                if not first:
                    add_out(b - 1)
                norm_apply(after, b + (NB + 1))
                dve.wait_ge(exp_made, b * 4 + 2)
                ch.done(dve.tensor_tensor_scan(bb[:, 1:1 + T], old_w[:, :], new_w[:, :], 0.0, ALU.mult, ALU.add))
                dve.wait_ge(kv_made, b * 2 + 1)
                dve.tensor_tensor_scan(aa[:, 1:1 + T], old_w[:, :], kv_w_new[:, :], 0.0, ALU.mult, ALU.add).then_inc(a_scanned, 1)
                dve.wait_ge(exp_made, b * 4 + 4)
                ch.wait()
                ch.link(dve.tensor_tensor(bb[:, 0:T], old_u[:, :], bb[:, 0:T], ALU.mult))
                ch.link(dve.tensor_tensor(den_u[:, :], bb[:, 0:T], new_u[:, :], ALU.add))
                dve.wait_ge(kvr_copied, b * 3 + 3)
                dve.scalar_tensor_tensor(out=p_out[:, :], in0=e_r[:, :], scalar=1.0, in1=den_u[:, :],
                                         op0=ALU.add, op1=ALU.mult).then_inc(div_made, 1)
                dve.wait_ge(kv_made, b * 2 + 2)
                dve.wait_ge(old_made, b + 1)
                ch.done(dve.tensor_tensor(kv_u_new[:, :], aa[:, 0:T], kv_u_new[:, :], ALU.add))
                dve.wait_ge(div_made, b + 1)
                if not more:
                    gate_scores(NB)
                ch.link(dve.reciprocal(p_out[:, :], p_out[:, :]))
                assert ch.n == WKV_CHAIN, ch.n
                dve.tensor_tensor(rw[:, :], kv_u_new[:, :], p_out[:, :], ALU.mult).then_inc(rw_made, 1)

            dve.wait_ge(cols_made, 2)
            dve.wait_ge(loaded, 16 * NLOAD)
            ffn(0)
            dve.wait_ge(ffn_done, NB - 1)
            mix_weights()
            norm_stats(0, NB)
            norm_apply(0, NB)
            time_mix(0, True, True)
            dve.wait_ge(ffn_done, NB)
            with dve.Fori(1, NB - 1) as b:
                time_mix(b, False, True)
            time_mix(NB - 1, False, False)
            add_out(NB - 1)
            ffn(1)
            b, ch = NB - 1, Chain(dve, last_chain, 0)
            xb = x[:, b * T:(b + 1) * T]
            for j in range(TOPK):
                dve.wait_ge(y_gathered[j], 2 * NB * NT * 16)
                y = y_got[:, j % 2, :].rearrange("p (n c) -> p n c", c=C)
                ch.link(dve.tensor_tensor(y, y, gate_now[:, j, :].unsqueeze(2).broadcast_to([P, NT, C]), ALU.mult))
                ch.link(dve.tensor_tensor(xb, xb, y_got[:, j % 2, :], ALU.add))
                if j == 0:
                    dve.sem_inc(y_used, 1)
            dve.sem_inc(last_done, 1)

        @block.tensor
        def _(pe):
            pe.wait_ge(loaded, 16 * NLOAD)
            pe.wait_ge(consts, NCONST)
            for i, w in enumerate((wq_raw, wk_raw)):
                for h in range(H):
                    pe.transpose(S[0:DH, i, h * C:(h + 1) * C], w[:, h * DH:(h + 1) * DH], ident[:, :])
            for i in range(4):
                ins = pe.transpose(TP[:, i * C:(i + 1) * C], rw_raw[:, i, :], ident[:, :])
            ins.then_inc(w_turned, 1)
            pe.wait_ge(w_copied, 3)
            for h in range(H):
                ins = pe.matmul(S[:, 0, h * C:(h + 1) * C], wkT[:, h, :], wqT[:, h, :], start=True, stop=True)
            ins.then_inc(g_made, 1)
            pe.wait_ge(g_copied, 1)
            pe.wait_ge(bias_made, 1 + NT * 16)

            def turn(r, halved=None):
                pe.wait_ge(xn_made, r + 1)
                for n in range(NT):
                    ins = pe.transpose(TP[:, n * P:(n + 1) * P], xn[:, n * C:(n + 1) * C], ident[:, :])
                    if halved is not None and n == NT // 2 - 1:
                        ins.then_inc(half_turned, 1)
                ins.then_inc(xn_turned, 1)

            def xT_tile(n):
                return xT[:, 1 + n * P:1 + (n + 1) * P]

            def logits(f):
                for n in range(NT):
                    ins = pe.matmul(logit_ps[:, n * H:(n + 1) * H], xT_tile(n), ws[:, :], start=True, stop=True)
                ins.then_inc(logits_made, 1)

            def ranks(f):
                pe.wait_ge(dense_made, f + 1)
                pe.sem_inc(passed, 1)
                pe.transpose(gT_ps, dense[:, :], ident[:, :]).then_inc(gT_turned, 1)
                pe.wait_ge(mask_made, f + 1)
                m = mask_b[:, :, :].rearrange("p n h -> p (n h)")
                pe.matmul(rank_ps, tri[:, :], m, start=True, stop=False, skip_group_check=True)
                for d in range(1, NT):
                    pe.matmul(rank_ps[:, d * H:NT * H], ones[:, :], m[:, 0:(NT - d) * H], start=False,
                              stop=(d == NT - 1), skip_group_check=True)
                for n in range(NT):
                    ins = pe.matmul(count_ps, ones[:, :], mask_b[:, n, :], start=(n == 0), stop=(n == NT - 1))
                ins.then_inc(rank_made, 1)

            def biases(f):
                pe.wait_ge(gT_made, f + 1)
                for i in range(2):
                    ins = pe.matmul(TP[:, i * 512:(i + 1) * 512], gT[:, :], bias[:, i * 512:(i + 1) * 512], start=True, stop=True)
                ins.then_inc(b_made, 1)

            def keys(f, heads):
                for h in heads:
                    if h >= 2:
                        pe.wait_ge(a_lo_made, f * H + (h - 1))
                    for i in range(2):
                        ins = pe.matmul(S[:, h % 2, i * 512:(i + 1) * 512], GT[:, h, :],
                                        xT[:, 1 + i * 512:1 + (i + 1) * 512], start=True, stop=True)
                    ins.then_inc(a_made, 1)

            def values(f, tiles):
                for n in tiles:
                    if n >= 2:
                        pe.wait_ge(v_lo_made, f * NT + (n - 1))
                    pe.matmul(TP[:, (n % 2) * 512:(n % 2) * 512 + 512], xT_tile(n), wv[:, :],
                              start=True, stop=True).then_inc(v_made, 1)

            def run(layer, b, f, more):
                r = f + (layer * NB + 1)
                pe.wait_ge(slots_made, f + 1)
                pe.sem_inc(passed, 1)

                def step(st):
                    a, q, p, o, y = (st.tile(c) for c in (AHEAD, SCORED, 0, -1, -BEHIND))
                    if p.live():
                        pe.wait_ge(p_made, f * NS + p.t + 1)
                        for i in range(2):
                            if more and st.s == TURN_STEP + 1:
                                if i == 0:
                                    pe.wait_ge(half_xT_made, f + (1 - layer))
                                else:
                                    pe.wait_ge(xT_made, r + 1)
                            if p.least >= 1:
                                pe.wait_ge(pT_lo_made, (f * NS + p.t) * 2 + (i - 1))
                            else:
                                pe.wait_ge(v_lo_made, (f + 1) * NT)
                            for n in range(4 * i, 4 * i + 4):
                                ins = pe.transpose(TP[:, n * P:(n + 1) * P], probs[:, p.par, n * P:(n + 1) * P], ident[:, :])
                            ins.then_inc(p_turned, 1)
                    if q.live():
                        in_A = pe.snap(head_on(pe, b, q.t) * T)
                    if q.live():
                        pe.wait_ge(xs_lo_made, f * NS + q.t + 1)
                        if q.least >= 2:
                            pe.wait_ge(p_made, f * NS + q.t - 1)
                        else:
                            pe.wait_ge(a_lo_made, (f + 1) * H)
                        for n, (xx, A) in enumerate(((xs_hi, A_hi), (xs_lo, A_hi), (xs_hi, A_lo))):
                            for i in range(2):
                                ins = pe.matmul(S[:, q.par, i * 512:(i + 1) * 512], xx[:, q.par, :],
                                                A[:, bass.ds(in_A + i * 512, 512)], start=(n == 0), stop=(n == 2))
                        ins.then_inc(s_made, 1)
                    if y.live():
                        in_wo = pe.snap(head_on(pe, b, y.t) * C)
                    if y.live():
                        pe.wait_ge(oT_made, f * NS + y.t + 1)
                        if y.least >= 1:
                            pe.wait_ge(y_copied, f * NS + y.t)
                    if a.least >= 1 and a.least <= NS:
                        pe.wait_ge(xs_lo_made, f * NS + a.t)
                    if more and st.s == LOGIT_STEP:
                        logits(f + 1)
                    if more and st.s == RANK_STEP:
                        ranks(f + 1)
                    if more and BIAS_STEP <= st.s < BIAS_STEP + NT:
                        if st.s == BIAS_STEP:
                            pe.wait_ge(gT_made, f + 2)
                        pe.matmul(b_ps, gT[:, :], bias[:, bass.ds((st.tile(-BIAS_STEP).t) * C, C)], start=True, stop=True)
                    if y.live():
                        pe.matmul(y_ps, oT[:, y.par, :], wo[:, bass.ds(in_wo, C)], start=True, stop=True).then_inc(y_made, 1)
                    if a.live():
                        pe.wait_ge(xs_loaded[a.par], (f * (16 - a.par) + a.same + 1) * 16)
                        pe.transpose(xT_ps, xs[:, a.par, :], ident[:, :]).then_inc(xs_turned, 1)
                    if o.live():
                        pe.wait_ge(pT_lo_made, (f * NS + o.t) * 2 + 2)
                        pe.wait_ge(v_now_made, f * NS + o.t + 1)
                        if o.least >= 1:
                            pe.wait_ge(oT_made, f * NS + o.t)
                        for n in range(NT):
                            ins = pe.matmul(o_ps, V_now[:, o.par, n * 2 * DH:(n + 1) * 2 * DH], pT[:, o.par, :, n * P:(n + 1) * P],
                                            start=(n == 0), stop=(n == NT - 1))
                        ins.then_inc(o_made, 1)
                    if st.s in VALUE_TILES:
                        values(f, VALUE_TILES[st.s])
                    if more and st.s >= KEY_STEP:
                        pe.wait_ge(p_made, (f + 1) * NS)
                        keys(f + 1, key_heads(st.s))
                    if more and st.s == TURN_STEP:
                        pe.wait_ge(pT_lo_made, (f * NS + (TURN_STEP + 1)) * 2)
                        turn(r, f + (1 - layer))

                pipeline(pe, step, lambda s: None)
                pe.wait_ge(y_copied, (f + 1) * NS)

            def ffn(layer):
                f0, r0 = layer * NB, 2 * layer * NB
                if layer == 0:
                    turn(r0)
                    pe.wait_ge(xT_made, r0 + 1)
                    logits(f0)
                    pe.wait_ge(eg_made, f0 + 1)
                ranks(f0)
                pe.wait_ge(rank_copied, f0 + 1)
                biases(f0)
                pe.wait_ge(b_added, (f0 + 1) * NT)
                keys(f0, range(H))
                runs(pe, layer, lambda b, f, more: run(layer, b, f, more))

            ffn(0)

            def turn_apart(b):
                pe.wait_ge(xn_made, b + (NB + 1))
                for n in range(NT):
                    bank = (OB, MB)[n // 4]
                    ins = pe.transpose(bank[:, (n % 4) * P:(n % 4 + 1) * P], xn[:, n * C:(n + 1) * C], ident[:, :])
                ins.then_inc(xn_turned, 1)
                pe.wait_ge(xT_made, b + (NB + 1))

            def front(b, first):
                turn_apart(b)
                for i, dst in enumerate((S[:, 0, :], S[:, 1, :], TP[:, :])):
                    if not first:
                        pe.wait_ge(kvr_copied, b * 3 + (i - 2))
                    for c in range(2):
                        pe.matmul(dst[:, c * 512:(c + 1) * 512], w_now[:, i * C:(i + 1) * C],
                                  xT[:, 1 + c * 512:1 + (c + 1) * 512], start=True, stop=False)
                        ins = pe.matmul(dst[:, c * 512:(c + 1) * 512], w_last[:, i * C:(i + 1) * C],
                                        xT[:, c * 512:(c + 1) * 512], start=False, stop=True)
                    ins.then_inc(kvr_made, 1)

            def out_rows(b):
                pe.wait_ge(rw_made, b + 1)
                for n in range(NT):
                    bank = (OB, MB)[n // 4]
                    ins = pe.matmul(bank[:, (n % 4) * C:(n % 4 + 1) * C], rw[:, n * P:(n + 1) * P], rw_T[:, 3, :],
                                    start=True, stop=True)
                ins.then_inc(ro_made, 1)

            pe.wait_ge(mix_made, 9)
            front(0, True)
            with pe.Fori(0, NB - 1) as b:
                front(b + 1, False)
                out_rows(b)
            turn_apart(NB)
            logits(NB)
            pe.wait_ge(eg_made, NB + 1)
            out_rows(NB - 1)
            pe.wait_ge(wkv_done, NB)
            ffn(1)


_INS = ['L0_attn_x', 'L0_attn_time_decay', 'L0_attn_time_first', 'L0_attn_time_mix_k', 'L0_attn_time_mix_v',
        'L0_attn_time_mix_r', 'L0_attn_Wk', 'L0_attn_Wv', 'L0_attn_Wr', 'L0_attn_Wo', 'L0_ffn_Wq', 'L0_ffn_Wkv',
        'L0_ffn_Ws', 'L0_ffn_Wo', 'L0_ffn_bo']
_OUTS = [((8, 1024, 128), 'float32')]


def kernel(**inputs):
    import numpy as _np
    import concourse.bacc as _bacc
    from concourse import mybir as _mybir
    from concourse.bass_utils import run_bass_kernel_spmd as _run

    nc = _bacc.Bacc("TRN2", target_bir_lowering=False, num_devices=1)
    arrays, args = {}, []
    for name in _INS:
        a = _np.ascontiguousarray(inputs[name])
        arrays[f"in_{name}_dram"] = a
        args.append(nc.dram_tensor(f"in_{name}_dram", a.shape, _mybir.dt.from_np(a.dtype), kind="ExternalInput").ap())
    for i, (shape, dtype) in enumerate(_OUTS):
        dt = _mybir.dt.from_np(_np.dtype(dtype))
        args.append(nc.dram_tensor(f"out_{i}_dram", shape, dt, kind="ExternalOutput").ap())
    build(nc, *args)
    r = _run(nc, [arrays], core_ids=[0])
    got = tuple(r.results[0][f"out_{i}_dram"] for i in range(len(_OUTS)))
    return got[0]
```
